# Optimizing a Trainium2 kernel written in Bass

```python
import numpy as np
import jax
import jax.numpy as jnp

def _softmax(x, axis=-1):
    return jax.nn.softmax(x, axis=axis)

def _gelu(x):
    return jax.nn.gelu(x, approximate=True)

def _silu(x):
    return jax.nn.silu(x)

def _sigmoid(x):
    return jax.nn.sigmoid(x)

def _layernorm(x, axis=-1, eps=1e-05):
    m = jnp.mean(x, axis=axis, keepdims=True)
    v = jnp.var(x, axis=axis, keepdims=True)
    return (x - m) / jnp.sqrt(v + eps)

def _scatter_add(tgt, idx, src, axis=0):
    return tgt.at[idx].add(src)

def _segment_sum(src, seg, n):
    return jax.ops.segment_sum(src, seg, n)
kernel_name = 'mk_recurrent_d1_jaxref_r8_6f15f0'

def setup_inputs(seed: int=0):
    np.random.seed(seed)
    _w = jnp.asarray

    def _L0_attn_setup():
        import jax, jax.numpy as jnp
        import numpy as np
        HEADS, KV_HEADS, HEAD_DIM = (16, 4, 128)
        WINDOW, ROPE_THETA, EPS = (64, 10000.0, 1e-06)

        def _rms_norm(x, w):
            xf = x.astype(jnp.float32)
            y = xf * jax.lax.rsqrt(jnp.mean(xf * xf, axis=-1, keepdims=True) + EPS)
            return (y * (1.0 + w.astype(jnp.float32))).astype(x.dtype)

        def _rope_cos_sin(T, dtype):
            inv_freq = 1.0 / ROPE_THETA ** (jnp.arange(0, HEAD_DIM, 2, dtype=jnp.float32) / HEAD_DIM)
            pos = jnp.arange(T, dtype=jnp.float32)
            freqs = pos[:, None] * inv_freq[None, :]
            emb = jnp.concatenate([freqs, freqs], axis=-1)
            return (emb.astype(dtype), emb)

        def _rotate_half(x):
            x1, x2 = jnp.split(x, 2, axis=-1)
            return jnp.concatenate([-x2, x1], axis=-1)
        key = jax.random.key(seed)
        ks = jax.random.split(key, 7)
        B, T, D = (2, 256, 256)
        s = lambda k, shape, fan: jax.random.normal(k, shape, jnp.float32) * fan ** (-0.5)
        return {'x': jax.random.normal(ks[0], (B, T, D), jnp.float32), 'Wq': s(ks[1], (HEADS * HEAD_DIM, D), D), 'Wk': s(ks[2], (KV_HEADS * HEAD_DIM, D), D), 'Wv': s(ks[3], (KV_HEADS * HEAD_DIM, D), D), 'Wo': s(ks[4], (D, HEADS * HEAD_DIM), HEADS * HEAD_DIM), 'qn_w': jax.random.normal(ks[5], (HEAD_DIM,), jnp.float32) * 0.02, 'kn_w': jax.random.normal(ks[6], (HEAD_DIM,), jnp.float32) * 0.02}
    _L0_attn_in = _L0_attn_setup()

    def _L0_ffn_setup():
        import jax, jax.numpy as jnp
        import numpy as np
        EPS = 1e-06
        K_STEPS = 4
        USE_GATING = True

        def layer_norm(x, gamma, beta):
            mu = jnp.mean(x, axis=-1, keepdims=True)
            var = jnp.mean(jnp.square(x - mu), axis=-1, keepdims=True)
            return (x - mu) * jax.lax.rsqrt(var + EPS) * gamma + beta
        key = jax.random.key(seed)
        B, L, D, H = (4, 512, 256, 1024)
        ks = jax.random.split(key, 16)
        s = 0.02
        return {'x': jax.random.normal(ks[0], (B, L, D), dtype=jnp.float32), 'in_gamma': jnp.ones((D,), jnp.float32), 'in_beta': jnp.zeros((D,), jnp.float32), 'agg_w': jax.random.normal(ks[1], (D, D), jnp.float32) * s, 'agg_b': jnp.zeros((D,), jnp.float32), 'pn_gamma': jnp.ones((D,), jnp.float32), 'pn_beta': jnp.zeros((D,), jnp.float32), 'd1_w': jax.random.normal(ks[2], (D, H), jnp.float32) * s, 'd1_b': jnp.zeros((H,), jnp.float32), 'd2_w': jax.random.normal(ks[3], (H, D), jnp.float32) * s, 'd2_b': jnp.zeros((D,), jnp.float32), 'bc_w': jax.random.normal(ks[4], (D, D), jnp.float32) * s, 'bc_b': jnp.zeros((D,), jnp.float32), 'gate_w': jax.random.normal(ks[5], (D, D), jnp.float32) * s, 'gate_b': jnp.zeros((D,), jnp.float32), 'out_gamma': jnp.ones((D,), jnp.float32), 'out_beta': jnp.zeros((D,), jnp.float32)}
    _L0_ffn_in = _L0_ffn_setup()
    _d = {'L0_attn_x': _L0_attn_in['x'], 'L0_attn_Wq': _L0_attn_in['Wq'], 'L0_attn_Wk': _L0_attn_in['Wk'], 'L0_attn_Wv': _L0_attn_in['Wv'], 'L0_attn_Wo': _L0_attn_in['Wo'], 'L0_attn_qn_w': _L0_attn_in['qn_w'], 'L0_attn_kn_w': _L0_attn_in['kn_w'], 'L0_ffn_in_gamma': _L0_ffn_in['in_gamma'], 'L0_ffn_in_beta': _L0_ffn_in['in_beta'], 'L0_ffn_agg_w': _L0_ffn_in['agg_w'], 'L0_ffn_agg_b': _L0_ffn_in['agg_b'], 'L0_ffn_pn_gamma': _L0_ffn_in['pn_gamma'], 'L0_ffn_pn_beta': _L0_ffn_in['pn_beta'], 'L0_ffn_d1_w': _L0_ffn_in['d1_w'], 'L0_ffn_d1_b': _L0_ffn_in['d1_b'], 'L0_ffn_d2_w': _L0_ffn_in['d2_w'], 'L0_ffn_d2_b': _L0_ffn_in['d2_b'], 'L0_ffn_bc_w': _L0_ffn_in['bc_w'], 'L0_ffn_bc_b': _L0_ffn_in['bc_b'], 'L0_ffn_gate_w': _L0_ffn_in['gate_w'], 'L0_ffn_gate_b': _L0_ffn_in['gate_b'], 'L0_ffn_out_gamma': _L0_ffn_in['out_gamma'], 'L0_ffn_out_beta': _L0_ffn_in['out_beta']}
    _x0 = _d['L0_attn_x']
    _d['L0_attn_x'] = jax.random.normal(jax.random.fold_in(jax.random.key(seed), 1), (2, 1024, 256), dtype=_x0.dtype)
    del _x0
    return _d

def reference(L0_attn_x, L0_attn_Wq, L0_attn_Wk, L0_attn_Wv, L0_attn_Wo, L0_attn_qn_w, L0_attn_kn_w, L0_ffn_in_gamma, L0_ffn_in_beta, L0_ffn_agg_w, L0_ffn_agg_b, L0_ffn_pn_gamma, L0_ffn_pn_beta, L0_ffn_d1_w, L0_ffn_d1_b, L0_ffn_d2_w, L0_ffn_d2_b, L0_ffn_bc_w, L0_ffn_bc_b, L0_ffn_gate_w, L0_ffn_gate_b, L0_ffn_out_gamma, L0_ffn_out_beta):

    def _L0_attn_ref(x, Wq, Wk, Wv, Wo, qn_w, kn_w):
        import jax, jax.numpy as jnp
        import numpy as np
        HEADS, KV_HEADS, HEAD_DIM = (16, 4, 128)
        WINDOW, ROPE_THETA, EPS = (64, 10000.0, 1e-06)

        def _rms_norm(x, w):
            xf = x.astype(jnp.float32)
            y = xf * jax.lax.rsqrt(jnp.mean(xf * xf, axis=-1, keepdims=True) + EPS)
            return (y * (1.0 + w.astype(jnp.float32))).astype(x.dtype)

        def _rope_cos_sin(T, dtype):
            inv_freq = 1.0 / ROPE_THETA ** (jnp.arange(0, HEAD_DIM, 2, dtype=jnp.float32) / HEAD_DIM)
            pos = jnp.arange(T, dtype=jnp.float32)
            freqs = pos[:, None] * inv_freq[None, :]
            emb = jnp.concatenate([freqs, freqs], axis=-1)
            return (emb.astype(dtype), emb)

        def _rotate_half(x):
            x1, x2 = jnp.split(x, 2, axis=-1)
            return jnp.concatenate([-x2, x1], axis=-1)
        B, T, D = x.shape
        H, Hkv, Dh = (HEADS, KV_HEADS, HEAD_DIM)
        G = H // Hkv
        q = (x @ Wq.T).reshape(B, T, H, Dh).transpose(0, 2, 1, 3)
        k = (x @ Wk.T).reshape(B, T, Hkv, Dh).transpose(0, 2, 1, 3)
        v = (x @ Wv.T).reshape(B, T, Hkv, Dh).transpose(0, 2, 1, 3)
        q = _rms_norm(q, qn_w)
        k = _rms_norm(k, kn_w)
        emb_c, emb_f = _rope_cos_sin(T, x.dtype)
        cos = jnp.cos(emb_f).astype(x.dtype)[None, None]
        sin = jnp.sin(emb_f).astype(x.dtype)[None, None]
        q = q * cos + _rotate_half(q) * sin
        k = k * cos + _rotate_half(k) * sin
        q = q * Dh ** (-0.5)
        qg = q.reshape(B, Hkv, G, T, Dh)
        scores = jnp.einsum('bhgtd,bhkd->bhgtk', qg.astype(jnp.float32), k.astype(jnp.float32))
        dist = jnp.arange(T)[:, None] - jnp.arange(T)[None, :]
        mask = (dist >= 0) & (dist <= WINDOW)
        scores = jnp.where(mask[None, None, None], scores, jnp.finfo(jnp.float32).min)
        att = jax.nn.softmax(scores, axis=-1).astype(x.dtype)
        ctx = jnp.einsum('bhgtk,bhkd->bhgtd', att, v)
        out = ctx.reshape(B, H, T, Dh).transpose(0, 2, 1, 3).reshape(B, T, H * Dh)
        return out @ Wo.T

    def _L0_ffn_ref(x, in_gamma, in_beta, agg_w, agg_b, pn_gamma, pn_beta, d1_w, d1_b, d2_w, d2_b, bc_w, bc_b, gate_w, gate_b, out_gamma, out_beta):
        import jax, jax.numpy as jnp
        import numpy as np
        EPS = 1e-06
        K_STEPS = 4
        USE_GATING = True

        def layer_norm(x, gamma, beta):
            mu = jnp.mean(x, axis=-1, keepdims=True)
            var = jnp.mean(jnp.square(x - mu), axis=-1, keepdims=True)
            return (x - mu) * jax.lax.rsqrt(var + EPS) * gamma + beta
        x_norm = layer_norm(x, in_gamma, in_beta)
        thought = x_norm[:, -1, :] @ agg_w + agg_b
        for _ in range(K_STEPS):
            t = layer_norm(thought, pn_gamma, pn_beta)
            t = jax.nn.gelu(t @ d1_w + d1_b, approximate=False)
            thought = thought + (t @ d2_w + d2_b)
        broadcast = (thought @ bc_w + bc_b)[:, None, :]
        if USE_GATING:
            gate = jax.nn.sigmoid(x @ gate_w + gate_b)
            out = x + gate * broadcast
        else:
            out = x + broadcast
        return layer_norm(out, out_gamma, out_beta)
    x = L0_attn_x
    xn = _layernorm(x, axis=-1)
    s = _L0_attn_ref(xn, L0_attn_Wq, L0_attn_Wk, L0_attn_Wv, L0_attn_Wo, L0_attn_qn_w, L0_attn_kn_w)
    g = _silu(_L0_ffn_ref(xn, L0_ffn_in_gamma, L0_ffn_in_beta, L0_ffn_agg_w, L0_ffn_agg_b, L0_ffn_pn_gamma, L0_ffn_pn_beta, L0_ffn_d1_w, L0_ffn_d1_b, L0_ffn_d2_w, L0_ffn_d2_b, L0_ffn_bc_w, L0_ffn_bc_b, L0_ffn_gate_w, L0_ffn_gate_b, L0_ffn_out_gamma, L0_ffn_out_beta))
    x = x + s * g
    return x

_drawn_inputs = setup_inputs


def setup_inputs(seed=0):
    import zlib

    import numpy as np

    out = dict(_drawn_inputs(seed))
    spreads = {'L0_ffn_in_gamma': (1.0, 0.6),
     'L0_ffn_in_beta': (0.0, 0.8),
     'L0_ffn_agg_b': (0.0, 2.0),
     'L0_ffn_pn_gamma': (1.0, 0.6),
     'L0_ffn_pn_beta': (0.0, 0.8),
     'L0_ffn_d1_b': (0.0, 0.8),
     'L0_ffn_d2_b': (0.0, 2.0),
     'L0_ffn_bc_b': (0.0, 2.0),
     'L0_ffn_gate_b': (0.0, 2.0),
     'L0_ffn_out_gamma': (1.0, 0.536),
     'L0_ffn_out_beta': (0.0, 0.594)}
    factors = {'L0_attn_qn_w': 8.0,
     'L0_attn_kn_w': 8.0,
     'L0_ffn_agg_w': 4.901,
     'L0_ffn_d1_w': 5.938,
     'L0_ffn_d2_w': 5.684,
     'L0_ffn_bc_w': 3.666,
     'L0_ffn_gate_w': 8.0}
    for name, (base, spread) in spreads.items():
        noise = np.random.default_rng([zlib.crc32(name.encode()), seed]).standard_normal(out[name].shape)
        drawn = base * np.exp(spread * noise) if base else spread * noise
        out[name] = jnp.asarray(drawn.astype(out[name].dtype))
    for name, factor in factors.items():
        out[name] = (out[name] * factor).astype(out[name].dtype)
    return out
```

```python
import concourse.bass as bass
from concourse import mybir
from contextlib import ExitStack

F32 = mybir.dt.float32
F32R = mybir.dt.float32r
BF16 = mybir.dt.bfloat16
ALU = mybir.AluOpType
ACT = mybir.ActivationFunctionType
AX = mybir.AxisListType

BATCH, T, D = 2, 1024, 256
HEADS, KV, DH = 16, 4, 128
G = HEADS // KV
WINDOW = 64
HID, K_STEPS = 1024, 4
TILES = BATCH * T // 128
STEPS = TILES * KV
DC = D // 128
HC = HID // 128
TPB = T // 128
PAIRS = TILES // 2
EPS_X, EPS_N, EPS_R = 1e-5, 1e-6, 1e-6
CH = 1024
Q_P, Q_K, Q_V, Q_G, JOBS = (0, 2, 4, 6), 1, 3, 5, 7


def build(nc, x, wq, wk, wv, wo, gw, aggw, d1w, d2w, bcw, cols, rows2, rows128, gbrow, rope, masks, sels, out):
    ctx = ExitStack()
    with ctx:
        def sb(name, shape, dt=F32):
            return ctx.enter_context(nc.sbuf_tensor(name, shape, dt))

        def pb(name, shape=(128, 512)):
            return ctx.enter_context(nc.psum_tensor(name, list(shape), F32))

        def sem(name):
            return ctx.enter_context(nc.semaphore(name))

        Wq = sb("Wq", [128, 2, KV, DC, 512], F32R)
        Wk = sb("Wk", [128, 2, DC, 512], F32R)
        Wv = sb("Wv", [128, 2, DC, 512], F32R)
        Wo = sb("Wo", [128, 2, HEADS, D], F32R)
        Wg = sb("Wg", [128, 2, DC, D], F32R)
        gb_part = sb("gb_part", [128, D], F32R)
        gb_sel = sb("gb_sel", [128, 128], F32R)
        store = sb("store", [128, 4 * CH])
        stage = [store[:, CH * k:CH * k + CH] for k in range(4)]
        t1 = [store[:, 512 * k:512 * k + 512] for k in (0, 1)]
        t2 = [store[:, 512 * k:512 * k + 512] for k in (2, 3)]
        qT = [store[:, 512 * k:512 * k + 512] for k in (4, 5)]
        prob = [store[:, 512 * k:512 * k + 512] for k in (6, 7)]
        cosq, sinq, cosk, sink = (sb(f"rope{k}", [128, TPB, DH]) for k in range(4))
        bc128 = sb("bc128", [128, 2 * D + 2 * DH])
        out_gamma, out_beta = bc128[:, 0:D], bc128[:, D:2 * D]
        maskt = sb("maskt", [128, 4, 2, 128], BF16)
        identf = sb("identf", [128, 128])
        identb = sb("identb", [128, 128], BF16)
        neghalf, eps_x, eps_n, eps_r = (sb(n, [128, 4]) for n in ("neghalf", "eps_x", "eps_n", "eps_r"))
        hb = sb("hb", [128, BATCH, D])
        d1_s = sb("d1_s", [128, DC, HID])
        d2_s = sb("d2_s", [128, HC, D])
        colv = sb("colv", [128, HC + 4 * DC])
        sel2 = sb("sel2", [2, BATCH, 128])
        fst = sb("fst", [2, 6])
        fmv = sb("fmv", [2, 2])
        fve = sb("fve", [2, 1])
        frs = sb("frs", [2, 1])
        tT = sb("tT", [128, DC, 2])
        zz = sb("zz", [128, HC, 2])
        hT = sb("hT", [128, HC, 2])
        late = sb("late", [128, 8 * D])
        gth, gu, gz, gsl, gy, so, gg = (late[:, D * k:D * k + D] for k in range(7))
        agg_s = late[:, 0:DC * D].rearrange("p (c d) -> p c d", c=DC)
        bc_s = late[:, DC * D:2 * DC * D].rearrange("p (c d) -> p c d", c=DC)
        fx, fy, th, thb = (late[0:2, D * k:D * k + D] for k in range(4, 8))
        xt = [sb(f"xt{k}", [128, D]) for k in (0, 1)]
        xr = [sb(f"xr{k}", [128, D]) for k in (0, 1)]
        xn = [sb(f"xn{k}", [128, D]) for k in (0, 1)]
        xT = [sb(f"xT{k}", [128, 2, DC, 128], F32R) for k in (0, 1)]
        kTb = [sb(f"kT{k}", [128, KV, 192]) for k in (0, 1)]
        Va = [sb(f"Va{k}", [128, 2, 512], F32R) for k in (0, 1)]
        Vb = [sb(f"Vb{k}", [128, 2, 512], F32R) for k in (0, 1)]
        kt1 = sb("kt1", [128, 512])
        kt2 = sb("kt2", [128, 512])
        gbr = kt1[0:64, 0:D]
        aggb, d2b, bcb = kt2[0:2, 0:D], kt2[0:2, D:2 * D], kt1[0:2, D:2 * D]
        kss = sb("kss", [128, KV])
        kr = sb("kr", [128, KV])
        kr2 = sb("kr2", [128, KV])
        junkk = sb("junkk", [128, 512], BF16)
        lst = sb("lst", [128, 6])
        lmv = sb("lmv", [128, 2])
        lve = sb("lve", [128, 1])
        lrs = sb("lrs", [128, 1])
        gst = sb("gst", [128, 6])
        gmv = sb("gmv", [128, 2])
        gve = sb("gve", [128, 1])
        grs = sb("grs", [128, 1])
        junk = sb("junk", [128, 512], BF16)
        ss = [sb(f"ss{k}", [128, G]) for k in (0, 1)]
        sse = [sb(f"sse{k}", [128, G]) for k in (0, 1)]
        rq = [sb(f"rq{k}", [128, G]) for k in (0, 1)]
        r2 = [sb(f"r2{k}", [128, 2, 2]) for k in (0, 1)]
        nmx = [sb(f"nmx{k}", [128, 4]) for k in (0, 1)]
        nb = [sb(f"nb{k}", [128, 4]) for k in (0, 1)]
        rsum = [sb(f"rsum{k}", [128, 4]) for k in (0, 1)]
        rinv = [sb(f"rinv{k}", [128, 4]) for k in (0, 1)]
        pT = [sb(f"pT{k}", [128, 2, 2, 2, 128], F32R) for k in (0, 1)]
        cT = [sb(f"cT{k}", [128, 2, G, 2, 64], F32R) for k in (0, 1)]

        gbh = cT[0][0:64, 0, 0:2].rearrange("p h u t -> p (h u t)")

        PA = [pb("pa0"), pb("pa1")]
        TR = [pb("tr0"), pb("tr1")]
        SC = [pb("sc0"), pb("sc1")]
        CT = pb("ct")
        OU = pb("ou")

        l_stage = [sem(f"l_stage{k}") for k in range(4)]
        l_b128, l_gb, l_sel, l_mask, l_ident, l_ffn, l_small = (
            sem(n) for n in ("l_b128", "l_gb", "l_sel", "l_mask", "l_ident", "l_ffn", "l_small"))
        l_x = [sem("l_x0"), sem("l_x1")]
        l_xr = [sem("l_xr0"), sem("l_xr1")]
        l_vlow = [sem("l_vlow0"), sem("l_vlow1")]
        l_vup = [sem("l_vup0"), sem("l_vup1")]
        st_out = [sem("st_out0"), sem("st_out1")]
        a_whi, d_wlo, p_init, d_tab, d_one = (sem(n) for n in ("a_whi", "d_wlo", "p_init", "d_tab", "d_one"))
        f_dve, f_act, f_pe, f_pool = sem("f_dve"), sem("f_act"), sem("f_pe"), sem("f_pool")
        f_link, f_mv, f_ve, f_thb = sem("f_link"), sem("f_mv"), sem("f_ve"), sem("f_thb")
        pe_xT, pe_pa, pe_T, pe_kT, pe_S, pe_X, pe_C, pe_O = (
            sem(n) for n in ("pe_xT", "pe_pa", "pe_T", "pe_kT", "pe_S", "pe_X", "pe_C", "pe_O"))
        a_xhi, a_qT, a_ssq, a_kss, a_vhi, a_kT, a_pt, a_exp, a_ct, a_gate, a_silu = (
            sem(n) for n in ("a_xhi", "a_qT", "a_ssq", "a_kss", "a_vhi", "a_kT", "a_pt", "a_exp", "a_ct",
                             "a_gate", "a_silu"))
        d_lst, d_lmv, d_xn, d_xlo, d_rope, d_krope, d_kadd, d_vlo, d_r2, d_mx, d_nb, d_pt, d_ct, d_rinv = (
            sem(n) for n in ("d_lst", "d_lmv", "d_xn", "d_xlo", "d_rope", "d_krope", "d_kadd", "d_vlo", "d_r2", "d_mx",
                             "d_nb", "d_pt", "d_ct", "d_rinv"))
        d_gu, d_gst, d_gmv, d_g1, d_g2, d_gg, d_out = (
            sem(n) for n in ("d_gu", "d_gst", "d_gmv", "d_g1", "d_g2", "d_gg", "d_out"))
        p_lve, p_lrs, p_add, p_sse, p_r, p_norm, p_kve, p_kr, p_k, p_gy, p_gve, p_grs, p_fin = (
            sem(n) for n in ("p_lve", "p_lrs", "p_add", "p_sse", "p_r", "p_norm", "p_kve", "p_kr",
                             "p_k", "p_gy", "p_gve", "p_grs", "p_fin"))

        chunks = [(wk, Wk[:, 0], Wk[:, 1]), (wv, Wv[:, 0], Wv[:, 1])]
        chunks += [(wq[:, g], Wq[:, 0, g], Wq[:, 1, g]) for g in range(KV)]
        chunks += [(gw, Wg[:, 0], Wg[:, 1])]
        chunks += [(wo[:, h:h + 4], Wo[:, 0, h:h + 4], Wo[:, 1, h:h + 4]) for h in range(0, HEADS, 4)]
        NW = len(chunks)
        NCH = NW + 2

        def width(src):
            n = 1
            for a in src.shape[1:]:
                n *= a
            return n

        def staged(k, like):
            return stage[k % 4][:, 0:width(like)].rearrange("p (a b) -> p a b", b=like.shape[-1])

        block = ctx.enter_context(nc.Block())

        def exists(s, lag=0):
            return not isinstance(s, int) or 0 <= s - lag < STEPS

        def tile_exists(n):
            return not isinstance(n, int) or 0 <= n < TILES

        def later(n, least=1):
            return not isinstance(n, int) or n >= least

        def wait(eng, s, n):
            if later(n):
                eng.wait_ge(s, n)

        def program(engine, slot):
            for k in range(8):
                slot(0, k, k)
            with engine.Fori(1, PAIRS - 1) as i:
                for k in range(8):
                    slot(i, k, 8 * i + k)
            for k in range(8 + 8):
                slot(PAIRS - 1 + k // 8, k % 8, 8 * (PAIRS - 1) + k)

        @block.sync
        def _(sp):
            sp.dma_start(fx[:, :], x[:, T - 1, :]).then_inc(l_small, 16)
            sp.dma_start(colv[:, :], cols).then_inc(l_small, 16)
            for k, dst in enumerate((aggb, d2b, bcb)):
                sp.dma_start(dst, rows2[D * k:D * k + D].partition_broadcast(2)).then_inc(l_small, 16)
            sp.dma_start(sel2[:, :, :], sels[0:2, 0:2 * 128].rearrange("p (a b) -> p a b", a=2)).then_inc(l_small, 16)
            sp.dma_start(xt[0][:, :], x[0, 0:128, :]).then_inc(l_x[0], 16)
            sp.dma_start(xt[1][:, :], x[0, 128:256, :]).then_inc(l_x[1], 16)
            sp.dma_start(identf[:, :], sels[:, 256:384]).then_inc(l_ident, 16)
            for dst, src in ((agg_s, aggw), (d1_s, d1w), (d2_s, d2w), (bc_s, bcw)):
                sp.dma_start(dst[:, :, :], src).then_inc(l_ffn, 16)
            sp.dma_start(bc128[:, :], rows128.partition_broadcast(128)).then_inc(l_b128, 16)
            sp.dma_start(gbr[0:1, :], gbrow).then_inc(l_gb, 16)
            sp.dma_start(gbr[32:33, :], gbrow).then_inc(l_gb, 16)
            sp.dma_start(maskt[:, 0:2, :, :], masks).then_inc(l_mask, 16)
            for k in range(NCH):
                if k >= 4:
                    sp.wait_ge(a_whi, min(k - 3, NW))
                    sp.wait_ge(d_wlo, min(k - 3, NW))
                if k < NW:
                    sp.dma_start(staged(k, chunks[k][0]), chunks[k][0]).then_inc(l_stage[k % 4], 16)
                else:
                    sp.dma_start(stage[k % 4].rearrange("p (m d) -> p m d", d=DH),
                                 rope[:, k - NW, :, :]).then_inc(l_stage[k % 4], 16)

            def slot(i, k, s):
                par, j, n = k // 4, k % 4, 2 * i + k // 4
                own = isinstance(i, int)
                if j == 0 and tile_exists(n) and (not own or n + 2 < TILES):
                    sp.wait_ge(d_xn, n + 1)
                    nxt = n + 2
                    sp.dma_start(xt[par][:, :], x.rearrange("b t d -> (b t) d")[bass.ds(nxt * 128, 128), :])\
                        .then_inc(l_x[par], 16)
                if j == 2 and tile_exists(n):
                    sp.wait_ge(d_vlo, n + 1)
                    wait(sp, pe_C, 4 * n - 4)
                    sp.dma_start(Vb[par][0:64, :, :].bitcast(F32), Va[par][0:64, :, :].bitcast(F32)).then_inc(l_vlow[par], 16)
                if j == 3 and tile_exists(n):
                    wait(sp, pe_C, 4 * n)
                    sp.wait_ge(d_vlo, n + 1)
                    sp.dma_start(Vb[1 - par][64:128, :, :].bitcast(F32), Va[par][64:128, :, :].bitcast(F32)).then_inc(l_vup[par], 16)
                if j == 3 and (not own or n >= 2):
                    sp.wait_ge(p_fin, n - 1)
                    prev = n - 2
                    sp.dma_start(out.rearrange("b t d -> (b t) d")[bass.ds(prev * 128, 128), :], xr[par][:, :])\
                        .then_inc(st_out[par], 16)
                if j == 3 and tile_exists(n):
                    if later(n, 2):
                        sp.wait_ge(st_out[par], 16 * i)
                    sp.dma_start(xr[par][:, :], x.rearrange("b t d -> (b t) d")[bass.ds(n * 128, 128), :])\
                        .then_inc(l_xr[par], 16)
            program(nc.sync, slot)
            for par in (0, 1):
                sp.wait_ge(l_vup[par], 16 * PAIRS)
                sp.wait_ge(st_out[par], 16 * PAIRS)

        @block.tensor
        def _(pe):

            def ffn_turn(dst, src, n_dve):
                pe.wait_ge(f_dve, n_dve)
                for c in range(DC):
                    last = nc.tensor.transpose(dst[:, 2 * c:2 * c + 2], src[:, 128 * c:128 * c + 128], identf[0:2, 0:2])
                last.then_inc(f_pe, 1)

            def rows(dst, lhs, w, chunks_n, n_dve):
                pe.wait_ge(f_dve, n_dve)
                for c in range(chunks_n):
                    last = nc.tensor.matmul(dst, lhs[:, c, :], w[:, c, :], start=(c == 0), stop=(c == chunks_n - 1))
                last.then_inc(f_pe, 1)

            pe.wait_ge(l_ident, 16)
            pe.wait_ge(l_small, 16 * 6)
            pe.wait_ge(l_ffn, 16 * 4)
            ffn_turn(TR[0], fy, 1)
            rows(TR[1][0:2, 0:D], tT, agg_s, DC, 2)
            for k in range(K_STEPS):
                ffn_turn(TR[0], fy, 3 + 3 * k)
                pe.wait_ge(f_dve, 4 + 3 * k)
                for m in range(HC):
                    for c in range(DC):
                        last = nc.tensor.matmul(SC[0][:, 2 * m:2 * m + 2], d1_s[:, c, 128 * m:128 * m + 128],
                                                tT[:, c, :], start=(c == 0), stop=(c == DC - 1))
                last.then_inc(f_pe, 1)
                pe.wait_ge(f_act, k + 1)
                rows(TR[1][0:2, 0:D], hT, d2_s, HC, 5 + 3 * k)
            ffn_turn(TR[0], th, 3 + 3 * K_STEPS)
            rows(TR[1][0:2, 0:D], tT, bc_s, DC, 4 + 3 * K_STEPS)
            pe.wait_ge(f_dve, 5 + 3 * K_STEPS)
            for b in range(BATCH):
                last = nc.tensor.matmul(SC[0][:, D * b:D * b + D], sel2[:, b, :], fy[:, :], start=True, stop=True)
            last.then_inc(f_pe, 1)

            def x_turn(n, par):
                pe.wait_ge(d_xn, n + 1)
                for c in range(DC):
                    last = nc.tensor.transpose(TR[1][:, 128 * c:128 * c + 128], xn[par][:, 128 * c:128 * c + 128],
                                               identf[:, :])
                last.then_inc(pe_xT, 1)

            def product(dst, par, w, start):
                for c in range(DC):
                    for p, q in ((0, 0), (0, 1), (1, 0)):
                        last = nc.tensor.matmul(dst, xT[par][:, p, c, :], w[:, q, c, :],
                                                start=(start and c == 0 and p + q == 0),
                                                stop=(c == DC - 1 and p == 1))
                last.then_inc(pe_pa, 1)

            pe.wait_ge(f_act, K_STEPS + 1)
            x_turn(0, 0)

            def slot(i, k, s):
                par, j, n = k // 4, k % 4, 2 * i + k // 4
                tr = {0: (0, 1), 1: (0, 1), 2: (0, 0), 3: (1, 0)}[j]
                first = isinstance(i, int) and i == 0
                if exists(s, 2):
                    t = s - 2
                    pe.wait_ge(p_add, t + 1)
                    if j == 0:
                        wait(pe, d_pt, t - 1)
                    if j in (1, 2):
                        wait(pe, a_qT, t)
                    if j == 3:
                        pe.wait_ge(a_kT, n + 1)
                    turned = TR[tr[0]][:, :].rearrange("p (a u e t) -> p a e u t", a=2, u=2, e=2)
                    for h in range(G):
                        last = nc.tensor.transpose(turned[:, h // 2, h % 2],
                                                   t1[(k - 2) % 2][:, 128 * h:128 * h + 128], identf[:, :])
                    last.then_inc(pe_T, 1)
                if j == 2 and tile_exists(n):
                    pe.wait_ge(p_k, n + 1)
                    wait(pe, d_pt, 4 * n - 1)
                    for h in range(KV):
                        last = nc.tensor.transpose(TR[1][:, 128 * h:128 * h + 128], kt1[:, 128 * h:128 * h + 128],
                                                   identf[:, :])
                    last.then_inc(pe_kT, 1)
                if exists(s, 5):
                    t = s - 5
                    jt, pt = (k - 5) % 4, ((k - 5) // 4) % 2
                    pe.wait_ge(d_ct, t + 1)
                    if jt == 0:
                        wait(pe, d_out, n - 1)
                    if isinstance(t, int) and t < KV:
                        pe.wait_ge(d_wlo, 2 + KV + 1 + jt + 1)
                    for h in range(G):
                        for p, q in ((0, 0), (0, 1), (1, 0)):
                            last = nc.tensor.matmul(OU[:, 0:D],
                                                    cT[(k - 5) % 2][:, p, h, :, :].rearrange("p u t -> p (u t)"),
                                                    Wo[:, q, G * jt + h, :],
                                                    start=(jt == 0 and h == 0 and p + q == 0),
                                                    stop=(jt == KV - 1 and h == G - 1 and p == 1))
                    last.then_inc(pe_O, 1)
                if exists(s, 2):
                    t = s - 2
                    jt, pt = (k - 2) % 4, ((k - 2) // 4) % 2
                    nt = n if j >= 2 else n - 1
                    it = i if k >= 2 else i - 1
                    pe.wait_ge(a_qT, t + 1)
                    pe.wait_ge(a_kT, nt + 1)
                    wait(pe, a_exp, t - 1)
                    if first:
                        pe.wait_ge(p_init, 6)
                        pe.wait_ge(d_one, 4)
                        pe.wait_ge(l_mask, 16)
                    bank = SC[k % 2]
                    if pt == 0:
                        mk = maskt[:, bass.ds(it % 4, 1), :, :]
                    else:
                        mk = maskt[:, 1:2, :, :]
                    nc.tensor.matmul(bank[:, :].rearrange("p (a u c) -> p a u c", a=2, u=2), identb[:, :],
                                     mk.to_broadcast([128, 2, 2, 128]), start=True, stop=False)
                    keys = kTb[pt][:, jt, :].rearrange("p (a c) -> p a c", c=64)
                    for p in range(2):
                        for u in range(2):
                            at = 128 * (2 * p + u)
                            kk = keys[:, 0:2, :] if u else keys[:, 0:3:2, :]
                            last = nc.tensor.matmul(bank[:, at:at + 128].rearrange("p (a c) -> p a c", a=2),
                                                    qT[k % 2][:, at:at + 128], kk, start=False,
                                                    stop=(p == 1 and u == 1))
                    last.then_inc(pe_S, 1)
                if exists(s, 3):
                    t = s - 3
                    pe.wait_ge(p_norm, t + 1)
                    if j == 0 and tile_exists(n):
                        pe.wait_ge(d_xlo, n + 1)
                    if j == 2 and tile_exists(n):
                        pe.wait_ge(a_qT, t + 2)
                    if j in (0, 2) and not tile_exists(n):
                        pe.wait_ge(a_qT, t + 1)
                    if j in (1, 3):
                        wait(pe, d_pt, t)
                    for c in range(4):
                        last = nc.tensor.transpose(TR[tr[1]][:, 128 * c:128 * c + 128],
                                                   prob[(k - 3) % 2][:, 128 * c:128 * c + 128], identf[:, :])
                    last.then_inc(pe_X, 1)
                if exists(s):
                    if first:
                        pe.wait_ge(d_wlo, 2 + j + 1)
                    if j == 0:
                        pe.wait_ge(d_xlo, n + 1)
                        wait(pe, a_gate, n)
                    else:
                        pe.wait_ge(a_ssq, s)
                    product(PA[(par + Q_P[j]) % 2][:, :], par, Wq[:, :, j], True)
                if tile_exists(n):
                    if j == 0:
                        if first:
                            pe.wait_ge(d_wlo, 1)
                        wait(pe, a_ssq, 4 * n)
                        product(PA[(par + Q_K) % 2][:, :], par, Wk, True)
                    if j == 1:
                        if first:
                            pe.wait_ge(d_wlo, 2)
                        pe.wait_ge(a_kss, n + 1)
                        product(PA[(par + Q_V) % 2][:, :], par, Wv, True)
                    if j == 2:
                        if first:
                            pe.wait_ge(d_wlo, 2 + KV + 1)
                            pe.wait_ge(d_one, 4)
                        pe.wait_ge(d_vlo, n + 1)
                        dst = PA[(par + Q_G) % 2][:, 0:D]
                        nc.tensor.matmul(dst, gb_sel[:, :], gb_part[:, :], start=True, stop=False)
                        product(dst, par, Wg, False)
                if j == 3 and tile_exists(n + 1):
                    pe.wait_ge(a_qT, 4 * n + 2)
                    x_turn(n + 1, 1 - par)
                if exists(s, 3):
                    t = s - 3
                    jt, pt = (k - 3) % 4, ((k - 3) // 4) % 2
                    pe.wait_ge(d_pt, t + 1)
                    it = i if k >= 3 else i - 1
                    pe.wait_ge(l_vlow[pt], 16 * (it + 1))
                    wait(pe, l_vup[1 - pt], 16 * (it + pt))
                    wait(pe, d_ct, t)
                    for u in range(2):
                        V = (Vb, Va)[u][pt]
                        for p, q in ((0, 0), (0, 1), (1, 0)):
                            last = nc.tensor.matmul(
                                CT[:, 256 * u:256 * u + 256].rearrange("p (a c) -> p a c", a=2),
                                V[:, p, DH * jt:DH * jt + DH], pT[(k - 3) % 2][:, q, :, u, :],
                                start=(p + q == 0), stop=(p == 1))
                    last.then_inc(pe_C, 1)
            program(nc.tensor, slot)

        @block.scalar
        def _(act):
            def w_hi(k):
                act.wait_ge(l_stage[k % 4], 16 * (k // 4 + 1))
                src, hi, _ = chunks[k]
                nc.scalar.activation(hi, staged(k, hi), ACT.Identity).then_inc(a_whi, 1)

            def x_hi(n, par):
                nc.scalar.activation(xT[par][:, 0, :, :], TR[1][:, 0:D].rearrange("p (c t) -> p c t", c=DC),
                                     ACT.Identity).then_inc(a_xhi, 1)

            done = 0
            for k in range(K_STEPS):
                for _ in range(3):
                    if done < NW:
                        w_hi(done)
                        done += 1
                act.wait_ge(f_dve, 5 + 3 * k)
                nc.scalar.activation(hT[:, :, :], zz[:, :, :], ACT.Gelu).then_inc(f_act, 1)
            act.wait_ge(f_pe, 2 + 3 * K_STEPS + 3)
            nc.scalar.activation(hb[:, :, :], SC[0][:, :].rearrange("p (b d) -> p b d", b=BATCH), ACT.Copy,
                                 scale=0.5).then_inc(f_act, 1)

            def slot(i, k, s):
                par, j, n = k // 4, k % 4, 2 * i + k // 4
                if j == 0 and tile_exists(n):
                    act.wait_ge(pe_xT, n + 1)
                    x_hi(n, par)
                if exists(s, 2):
                    t = s - 2
                    act.wait_ge(pe_T, t + 1)
                    wait(act, pe_S, t - 1)
                    nc.scalar.activation(qT[k % 2], TR[1 if j == 3 else 0][:, :], ACT.Identity).then_inc(a_qT, 1)
                if j == 2 and tile_exists(n):
                    act.wait_ge(pe_kT, n + 1)
                    src = TR[1][:, :].rearrange("p (h t) -> p h t", h=KV)
                    nc.scalar.activation(kTb[par][:, :, 0:128], src, ACT.Identity)
                    nc.scalar.activation(kTb[1 - par][:, :, 128:192], src[:, :, 64:128], ACT.Identity).then_inc(a_kT, 1)
                if exists(s, 4):
                    t = s - 4
                    act.wait_ge(pe_C, t + 1)
                    wait(act, pe_O, t - 1)
                    nc.scalar.activation(cT[k % 2][:, 0].rearrange("p h u t -> p u h t"),
                                         CT[:, :].rearrange("p (u h t) -> p u h t", u=2, h=G),
                                         ACT.Identity).then_inc(a_ct, 1)
                if exists(s, 1):
                    t = s - 1
                    jt, pt = (k - 1) % 4, ((k - 1) // 4) % 2
                    act.wait_ge(d_rope, t + 1)
                    wait(act, p_sse, t - 1)
                    wait(act, a_ssq, t)
                    for h in range(G):
                        last = nc.scalar.activation(junk[:, 128 * h:128 * h + 128],
                                                    PA[(pt + Q_P[jt]) % 2][:, 128 * h:128 * h + 128], ACT.Square,
                                                    accum_out=ss[(k - 1) % 2][:, h:h + 1])
                    last.then_inc(a_ssq, 1)
                if j == 1 and tile_exists(n):
                    act.wait_ge(d_krope, n + 1)
                    wait(act, p_kve, n)
                    wait(act, a_kss, n)
                    for h in range(KV):
                        last = nc.scalar.activation(junkk[:, 128 * h:128 * h + 128],
                                                    PA[(par + Q_K) % 2][:, 128 * h:128 * h + 128], ACT.Square,
                                                    accum_out=kss[:, h:h + 1])
                    last.then_inc(a_kss, 1)
                if j == 2 and tile_exists(n):
                    act.wait_ge(pe_pa, JOBS * n + Q_V + 1)
                    wait(act, l_vlow[par], 16 * i)
                    wait(act, l_vup[par], 16 * i)
                    wait(act, pe_C, 4 * n - 4)
                    nc.scalar.activation(Va[par][:, 0, :], PA[(par + Q_V) % 2][:, :], ACT.Identity).then_inc(a_vhi, 1)
                if j == 3 and tile_exists(n):
                    act.wait_ge(pe_pa, JOBS * n + Q_G + 1)
                    wait(act, d_gu, n)
                    nc.scalar.activation(gth[:, :], PA[(par + Q_G) % 2][:, 0:D], ACT.Tanh, scale=0.5).then_inc(a_gate, 1)
                if exists(s, 3):
                    t = s - 3
                    act.wait_ge(pe_X, t + 1)
                    wait(act, pe_C, t - 1)
                    nc.scalar.activation(pT[(k - 3) % 2][:, 0],
                                         TR[0 if j >= 2 else 1][:, :].rearrange("p (a u c) -> p a u c", a=2, u=2),
                                         ACT.Identity).then_inc(a_pt, 1)
                if exists(s, 2):
                    t = s - 2
                    act.wait_ge(d_nb, t + 1)
                    wait(act, pe_X, t - 1)
                    for c in range(4):
                        last = nc.scalar.activation(prob[k % 2][:, 128 * c:128 * c + 128],
                                                    SC[k % 2][:, 128 * c:128 * c + 128], ACT.Exp,
                                                    bias=nb[k % 2][:, c:c + 1], scale=r2[k % 2][:, c // 2, c % 2:c % 2 + 1],
                                                    accum_out=rsum[k % 2][:, c:c + 1])
                    last.then_inc(a_exp, 1)
                if j == 3 and tile_exists(n - 1):
                    act.wait_ge(d_g2, n)
                    wait(act, d_gg, n - 1)
                    nc.scalar.activation(gsl[:, :], gz[:, :], ACT.Tanh, scale=0.5).then_inc(a_silu, 1)
            program(nc.scalar, slot)

        @block.gpsimd
        def _(pool):
            def rsqrt(dst, tmp, src, eps, s_tmp, n_tmp, s_dst):
                p, w = tmp.shape[0], tmp.shape[-1]
                nc.gpsimd.tensor_tensor(tmp, src, eps[0:p, 0:w], ALU.add).then_inc(s_tmp, 1)
                pool.wait_ge(s_tmp, n_tmp)
                nc.gpsimd.tensor_tensor(dst, tmp, neghalf[0:p, 0:w], ALU.pow).then_inc(s_dst, 1)

            nc.gpsimd.memset(eps_x[:, :], EPS_X)
            nc.gpsimd.memset(eps_n[:, :], EPS_N)
            nc.gpsimd.memset(eps_r[:, :], DH * EPS_R)
            nc.gpsimd.memset(neghalf[:, :], -0.5).then_inc(p_init, 1)
            nc.gpsimd.memset(kTb[0][:, :, 128:192], 0.0).then_inc(p_init, 1)
            nc.gpsimd.memset(Vb[0][:, :, :].bitcast(F32), 0.0).then_inc(p_init, 1)
            nc.gpsimd.memset(gb_part[:, :].bitcast(F32), 0.0).then_inc(p_init, 1)
            nc.gpsimd.memset(gb_sel[:, :].bitcast(F32), 0.0).then_inc(p_init, 1)
            pool.wait_ge(p_init, 5)
            pool.wait_ge(l_mask, 16)
            nc.gpsimd.tensor_copy(maskt[:, 2:4, :, :], maskt[:, 1:2, :, :].to_broadcast([128, 2, 2, 128]))\
                .then_inc(p_init, 1)
            pool.wait_ge(d_lmv, 1)
            rsqrt(lrs[:, :], lve[:, :], lmv[:, 1:2], eps_x, p_lve, 1, p_lrs)
            for k in range(2 + K_STEPS):
                pool.wait_ge(f_mv, k + 1)
                rsqrt(frs[:, :], fve[:, :], fmv[:, 1:2], eps_n if k else eps_x, f_ve, k + 1, f_pool)

            def slot(i, k, s):
                par, j, n = k // 4, k % 4, 2 * i + k // 4
                if exists(s, 3):
                    t = s - 3
                    pool.wait_ge(d_rinv, t + 1)
                    p3 = prob[(k - 3) % 2].rearrange("p (c n) -> p c n", c=4)
                    nc.gpsimd.tensor_tensor(p3, p3, rinv[(k - 3) % 2][:, :].unsqueeze(2).to_broadcast([128, 4, 128]),
                                            ALU.mult).then_inc(p_norm, 1)
                if exists(s, 1):
                    t = s - 1
                    q = (k - 1) % 2
                    pool.wait_ge(d_rope, t + 1)
                    nc.gpsimd.tensor_tensor(t1[q], t1[q], t2[q], ALU.add).then_inc(p_add, 1)
                    pool.wait_ge(a_ssq, t + 1)
                    wait(pool, d_r2, t - 1)
                    rsqrt(rq[q][:, :], sse[q][:, :], ss[q][:, :], eps_r, p_sse, t + 1, p_r)
                if j == 0 and tile_exists(n - 1):
                    pool.wait_ge(d_gu, n)
                    wait(pool, d_g1, n - 1)
                    nc.gpsimd.tensor_tensor(gy[:, :], gu[:, :], xn[1 - par][:, :], ALU.add).then_inc(p_gy, 1)
                if j == 0 and tile_exists(n + 1):
                    pool.wait_ge(d_lmv, n + 2)
                    rsqrt(lrs[:, :], lve[:, :], lmv[:, 1:2], eps_x, p_lve, n + 2, p_lrs)
                if j == 1 and tile_exists(n):
                    pool.wait_ge(a_kss, n + 1)
                    rsqrt(kr2[:, :], kr[:, :], kss[:, :], eps_r, p_kve, n + 1, p_kr)
                    pool.wait_ge(d_kadd, n + 1)
                    pool.wait_ge(p_kr, n + 1)
                    k3 = kt1[:, :].rearrange("p (h d) -> p h d", h=KV)
                    nc.gpsimd.tensor_tensor(k3, k3, kr2[:, :].unsqueeze(2).to_broadcast([128, KV, DH]),
                                            ALU.mult).then_inc(p_k, 1)
                if j == 2 and tile_exists(n - 1):
                    pool.wait_ge(d_gmv, n)
                    rsqrt(grs[:, :], gve[:, :], gmv[:, 1:2], eps_n, p_gve, n, p_grs)
                if j == 3 and (not isinstance(n, int) or n >= 2):
                    pool.wait_ge(d_out, n - 1)
                    pool.wait_ge(l_xr[par], 16 * i)
                    nc.gpsimd.tensor_tensor(xr[par][:, :], so[:, :], xr[par][:, :], ALU.add).then_inc(p_fin, 1)
            program(nc.gpsimd, slot)

        @block.vector
        def _(dve):
            chain = [0]

            def link(ins):
                chain[0] += 1
                ins.then_inc(f_link, 1)
                dve.wait_ge(f_link, chain[0])

            def w_lo(k):
                dve.wait_ge(a_whi, k + 1)
                src, hi, lo = chunks[k]
                nc.vector.tensor_tensor(lo, staged(k, lo), hi.bitcast(F32), ALU.subtract).then_inc(d_wlo, 1)

            def x_lo(n, par):
                dve.wait_ge(a_xhi, n + 1)
                nc.vector.tensor_tensor(xT[par][:, 1, :, :], TR[1][:, 0:D].rearrange("p (c t) -> p c t", c=DC),
                                        xT[par][:, 0, :, :].bitcast(F32), ALU.subtract).then_inc(d_xlo, 1)

            def x_stats(n, par):
                nc.vector.bn_stats(lst[:, :], xt[par][:, :]).then_inc(d_lst, 1)
                dve.wait_ge(l_x[0], 16)
                dve.wait_ge(d_lst, n)
                nc.vector.bn_aggr(lmv[:, :], lst[:, :]).then_inc(d_lmv, 1)

            def x_norm(n, par):
                dve.wait_ge(p_lrs, n + 1)
                dve.wait_ge(d_lmv, n + 1)
                nc.vector.tensor_scalar(xn[par][:, :], xt[par][:, :], lmv[:, 0:1], lrs[:, 0:1], ALU.subtract,
                                        ALU.mult).then_inc(d_xn, 1)

            dve.wait_ge(l_x[0], 16)
            link(nc.vector.bn_stats(lst[:, :], xt[0][:, :]))
            nc.vector.bn_aggr(lmv[:, :], lst[:, :]).then_inc(d_lmv, 1)
            dve.wait_ge(l_ident, 16)
            nc.vector.tensor_copy(identb[:, :], identf[:, :]).then_inc(d_one, 1)
            x_norm(0, 0)

            norms = [0]

            def ffn_norm(dst, src):
                link(nc.vector.bn_stats(fst[:, :], src[:, :]))
                norms[0] += 1
                nc.vector.bn_aggr(fmv[:, :], fst[:, :]).then_inc(f_mv, 1)
                dve.wait_ge(f_mv, norms[0])
                dve.wait_ge(f_pool, norms[0])
                return nc.vector.tensor_scalar(dst[:, :], src[:, :], fmv[:, 0:1], frs[:, 0:1], ALU.subtract, ALU.mult)

            def ffn_cols(gamma, beta, n_pe):
                dve.wait_ge(f_pe, n_pe)
                for c in range(DC):
                    src = TR[0][:, 2 * c:2 * c + 2]
                    if gamma is None:
                        last = nc.vector.tensor_copy(tT[:, c, :], src)
                    else:
                        last = nc.vector.tensor_scalar(tT[:, c, :], src, colv[:, gamma + c:gamma + c + 1],
                                                       colv[:, beta + c:beta + c + 1], ALU.mult, ALU.add)
                last.then_inc(f_dve, 1)

            done = [0]

            def some(k):
                for _ in range(k):
                    if done[0] < NW:
                        w_lo(done[0])
                        done[0] += 1

            ING, INB, PNG, PNB = (HC + DC * k for k in range(4))
            dve.wait_ge(l_small, 16 * 6)
            link(ffn_norm(fx, fx))
            ffn_norm(fy, fx).then_inc(f_dve, 1)
            ffn_cols(ING, INB, 1)
            dve.wait_ge(f_pe, 2)
            link(nc.vector.tensor_tensor(th[:, :], TR[1][0:2, 0:D], aggb, ALU.add))
            for k in range(K_STEPS):
                dve.wait_ge(f_dve, 2 + 3 * k)
                ffn_norm(fy, th).then_inc(f_dve, 1)
                nc.vector.tensor_tensor(thb[:, :], th[:, :], d2b, ALU.add).then_inc(f_thb, 1)
                ffn_cols(PNG, PNB, 3 + 3 * k)
                some(1)
                dve.wait_ge(f_pe, 4 + 3 * k)
                nc.vector.tensor_tensor(zz[:, :, :], SC[0][:, 0:2 * HC].rearrange("p (m b) -> p m b", b=2),
                                        colv[:, 0:HC].unsqueeze(2).to_broadcast([128, HC, 2]), ALU.add).then_inc(f_dve, 1)
                some(2)
                dve.wait_ge(f_thb, k + 1)
                dve.wait_ge(f_pe, 5 + 3 * k)
                last = nc.vector.tensor_tensor(th[:, :], TR[1][0:2, 0:D], thb[:, :], ALU.add)
                if k < K_STEPS - 1:
                    link(last)
                else:
                    last.then_inc(f_dve, 1)
            ffn_cols(None, None, 3 + 3 * K_STEPS)
            dve.wait_ge(f_pe, 4 + 3 * K_STEPS)
            nc.vector.tensor_tensor(fy[:, :], TR[1][0:2, 0:D], bcb, ALU.add).then_inc(f_dve, 1)
            some(NW)
            dve.wait_ge(l_gb, 32)
            dve.wait_ge(p_init, 5)
            link(nc.vector.tensor_copy(gbh[32:33, :], gbr[32:33, :]))
            nc.vector.tensor_copy(gb_part[0:1, :], gbr[0:1, :])
            nc.vector.tensor_tensor(gb_part[32:33, :], gbr[32:33, :], gbh[32:33, :].bitcast(F32), ALU.subtract)
            nc.vector.memset(gb_sel[0:1, :].bitcast(F32), 1.0)
            nc.vector.memset(gb_sel[32:33, :].bitcast(F32), 1.0).then_inc(d_one, 3)
            dve.wait_ge(l_b128, 16)
            w1 = bc128[:, 2 * D:2 * D + 2 * DH]
            w1q, w1k = w1[:, 0:DH], w1[:, DH:2 * DH]
            nc.vector.tensor_scalar(w1q, w1q, 1.0, None, ALU.add)
            link(nc.vector.tensor_scalar(w1k, w1k, 1.0, DH ** 0.5, ALU.add, ALU.mult))
            for part, tabs in ((0, (cosq, cosk)), (1, (sinq, sink))):
                c = NW + part
                dve.wait_ge(l_stage[c % 4], 16 * (c // 4 + 1))
                raw = stage[c % 4].rearrange("p (m a d) -> p m a d", a=2, d=DH // 2)
                for q, tab in enumerate(tabs):
                    w = w1[:, DH * q:DH * q + DH].rearrange("p (a d) -> p a d", a=2)
                    if part:
                        w = w[:, ::-1, :]
                    last = nc.vector.tensor_tensor(tab[:, :, :].rearrange("p m (a d) -> p m a d", a=2), raw,
                                                   w.unsqueeze(1).to_broadcast([128, TPB, 2, DH // 2]), ALU.mult)
            last.then_inc(d_tab, 1)
            dve.wait_ge(d_tab, 1)
            dve.wait_ge(d_wlo, NW)

            def rotate(dst_c, dst_s, bank, cos, sin, m):
                c = cos[:, bass.ds(m, 1), :].to_broadcast([128, 4, DH])
                q = sin[:, bass.ds(m, 1), :].rearrange("p m (a d) -> p m a d", a=2).to_broadcast([128, 4, 2, DH // 2])
                nc.vector.tensor_tensor(dst_c.rearrange("p (h d) -> p h d", h=4),
                                        bank.rearrange("p (h d) -> p h d", h=4), c, ALU.mult)
                return nc.vector.tensor_tensor(dst_s.rearrange("p (h a d) -> p h a d", h=4, a=2),
                                               bank.rearrange("p (h a d) -> p h a d", h=4, a=2)[:, :, ::-1, :], q,
                                               ALU.mult)

            def slot(i, k, s):
                par, j, n = k // 4, k % 4, 2 * i + k // 4
                if j == 0 and tile_exists(n):
                    x_lo(n, par)
                if exists(s, 3):
                    t = s - 3
                    dve.wait_ge(a_exp, t + 1)
                    wait(dve, p_norm, t - 1)
                    nc.vector.reciprocal(rinv[(k - 3) % 2][:, :], rsum[(k - 3) % 2][:, :]).then_inc(d_rinv, 1)
                if exists(s, 1):
                    t = s - 1
                    jt, pt = (k - 1) % 4, ((k - 1) // 4) % 2
                    it = i if k >= 1 else i - 1
                    nt = 2 * it + pt
                    dve.wait_ge(pe_pa, JOBS * nt + Q_P[jt] + 1)
                    wait(dve, pe_T, t - 1)
                    rotate(t1[(k - 1) % 2], t2[(k - 1) % 2], PA[(pt + Q_P[jt]) % 2][:, :], cosq, sinq,
                           (it % 4) * 2 + pt).then_inc(d_rope, 1)
                if j == 0 and tile_exists(n - 1):
                    it = i if par else i - 1
                    dve.wait_ge(a_gate, n)
                    wait(dve, p_gy, n - 1)
                    nc.vector.scalar_tensor_tensor(out=gu[:, :], in0=gth[:, :], scalar=1.0,
                                                   in1=hb[:, bass.ds(it // 4, 1), :].rearrange("p b d -> p (b d)"),
                                                   op0=ALU.add, op1=ALU.mult).then_inc(d_gu, 1)
                if j == 1 and tile_exists(n):
                    dve.wait_ge(pe_pa, JOBS * n + Q_K + 1)
                    wait(dve, pe_kT, n)
                    rotate(kt1[:, :], kt2[:, :], PA[(par + Q_K) % 2][:, :], cosk, sink, (i % 4) * 2 + par)\
                        .then_inc(d_krope, 1)
                if exists(s, 4):
                    t = s - 4
                    dve.wait_ge(a_ct, t + 1)
                    nc.vector.tensor_tensor(cT[k % 2][:, 1].rearrange("p h u t -> p u h t"),
                                            CT[:, :].rearrange("p (u h t) -> p u h t", u=2, h=G),
                                            cT[k % 2][:, 0].rearrange("p h u t -> p u h t").bitcast(F32),
                                            ALU.subtract).then_inc(d_ct, 1)
                if exists(s, 2):
                    t = s - 2
                    dve.wait_ge(pe_S, t + 1)
                    wait(dve, a_exp, t - 1)
                    nc.vector.tensor_reduce(nmx[k % 2][:, :], SC[k % 2][:, :].rearrange("p (c n) -> p c n", c=4), AX.X,
                                            ALU.max, negate=True).then_inc(d_mx, 1)
                if j == 1 and tile_exists(n):
                    dve.wait_ge(d_krope, n + 1)
                    nc.vector.tensor_tensor(kt1[:, :], kt1[:, :], kt2[:, :], ALU.add).then_inc(d_kadd, 1)
                if j == 2 and tile_exists(n):
                    dve.wait_ge(a_vhi, n + 1)
                    nc.vector.tensor_tensor(Va[par][:, 1, :], PA[(par + Q_V) % 2][:, :], Va[par][:, 0, :].bitcast(F32),
                                            ALU.subtract).then_inc(d_vlo, 1)
                if exists(s, 2):
                    dve.wait_ge(p_r, t + 1)
                    for hh in range(2):
                        for u in range(2):
                            last = nc.vector.tensor_copy(r2[k % 2][64 * hh:64 * hh + 64, :, u],
                                                         rq[k % 2][64 * u:64 * u + 64, hh::2])
                    last.then_inc(d_r2, 1)
                    dve.wait_ge(d_mx, t + 1)
                    dve.wait_ge(d_r2, t + 1)
                    nc.vector.tensor_tensor(nb[k % 2][:, :], nmx[k % 2][:, :],
                                            r2[k % 2][:, :, :].rearrange("p a u -> p (a u)"), ALU.mult).then_inc(d_nb, 1)
                if exists(s, 3):
                    t = s - 3
                    dve.wait_ge(a_pt, t + 1)
                    nc.vector.tensor_tensor(pT[(k - 3) % 2][:, 1],
                                            TR[0 if j >= 2 else 1][:, :].rearrange("p (a u c) -> p a u c", a=2, u=2),
                                            pT[(k - 3) % 2][:, 0].bitcast(F32), ALU.subtract).then_inc(d_pt, 1)
                if j == 0 and (not isinstance(n, int) or (2 <= n < TILES + 2)):
                    dve.wait_ge(a_silu, n - 1)
                    wait(dve, d_out, n - 2)
                    nc.vector.scalar_tensor_tensor(out=gg[:, :], in0=gsl[:, :], scalar=1.0, in1=gz[:, :],
                                                   op0=ALU.add, op1=ALU.mult).then_inc(d_gg, 1)
                    dve.wait_ge(pe_O, 4 * n - 4)
                    dve.wait_ge(d_gg, n - 1)
                    wait(dve, p_fin, n - 2)
                    nc.vector.scalar_tensor_tensor(out=so[:, :], in0=OU[:, 0:D], scalar=0.5,
                                                   in1=gg[:, :], op0=ALU.mult, op1=ALU.mult).then_inc(d_out, 1)
                if j == 0 and tile_exists(n + 1):
                    dve.wait_ge(l_x[1 - par], 16 * (i + 1 + par))
                    dve.wait_ge(d_xn, n + 1)
                    x_stats(n + 1, 1 - par)
                if j == 1 and tile_exists(n - 1):
                    dve.wait_ge(p_gy, n)
                    wait(dve, d_g2, n - 1)
                    nc.vector.bn_stats(gst[:, :], gy[:, :]).then_inc(d_gst, 1)
                    dve.wait_ge(l_x[0], 16)
                    dve.wait_ge(d_gst, n)
                    nc.vector.bn_aggr(gmv[:, :], gst[:, :]).then_inc(d_gmv, 1)
                if j == 2 and tile_exists(n + 1):
                    if later(n, 1):
                        dve.wait_ge(p_gy, n)
                    x_norm(n + 1, 1 - par)
                if j == 3 and tile_exists(n - 1):
                    dve.wait_ge(p_grs, n)
                    dve.wait_ge(d_gmv, n)
                    wait(dve, d_gg, n - 1)
                    nc.vector.scalar_tensor_tensor(out=gz[:, :], in0=gy[:, :], scalar=gmv[:, 0:1], in1=out_gamma,
                                                   op0=ALU.subtract, op1=ALU.mult).then_inc(d_g1, 1)
                    dve.wait_ge(d_g1, n)
                    nc.vector.scalar_tensor_tensor(out=gz[:, :], in0=gz[:, :], scalar=grs[:, 0:1], in1=out_beta,
                                                   op0=ALU.mult, op1=ALU.add).then_inc(d_g2, 1)
            program(nc.vector, slot)


def kernel(**inputs):
    import numpy as np
    import ml_dtypes
    import concourse.bacc as bacc
    from concourse.bass_utils import run_bass_kernel_spmd as run

    a = {k.replace("L0_attn_", "").replace("L0_ffn_", "f_"): np.asarray(v) for k, v in inputs.items()}

    def parts(w, c=DC):
        return np.ascontiguousarray(w.reshape(c, 128, -1).transpose(1, 0, 2))

    def col(v):
        return v.reshape(-1, 128).T

    arrays = {
        "x": np.ascontiguousarray(a["x"]),
        "wq": np.ascontiguousarray(a["Wq"].T.reshape(DC, 128, KV, 512).transpose(1, 2, 0, 3)),
        "wk": parts(a["Wk"].T),
        "wv": parts(a["Wv"].T),
        "wo": parts(a["Wo"].T, HEADS),
        "gw": parts(a["f_gate_w"]),
        "aggw": parts(a["f_agg_w"]),
        "d1w": parts(a["f_d1_w"]),
        "d2w": parts(a["f_d2_w"], HC),
        "bcw": parts(a["f_bc_w"]),
        "cols": np.ascontiguousarray(np.concatenate(
            [col(a["f_" + k]) for k in ("d1_b", "in_gamma", "in_beta", "pn_gamma", "pn_beta")], axis=1)),
        "rows2": np.concatenate([a["f_agg_b"], a["f_d2_b"], a["f_bc_b"]]),
        "rows128": np.concatenate([a["f_out_gamma"], a["f_out_beta"], a["qn_w"], a["kn_w"]]),
        "gbrow": np.ascontiguousarray(a["f_gate_b"].reshape(1, D)),
    }
    inv = np.float32(1.0) / np.float32(10000.0) ** (np.arange(0, DH, 2, dtype=np.float32) / np.float32(DH))
    ang = np.arange(T, dtype=np.float32)[:, None] * inv[None, :].astype(np.float32)
    cos, sin = np.cos(ang), np.sin(ang)
    rope = np.stack([np.concatenate([cos, cos], 1), np.concatenate([-sin, sin], 1)])
    arrays["rope"] = np.ascontiguousarray(rope.reshape(2, TPB, 128, DH).transpose(2, 0, 1, 3).astype(np.float32))
    tok, key = np.arange(128)[:, None] % 64, np.arange(128)[None, :]
    second = (key >= tok) & (key <= tok + WINDOW)
    before = (key >= 64) & (key >= tok + 64)
    same = (key < 64) & (key <= tok)
    masks = np.stack([np.stack([same, second]), np.stack([same | before, second])])
    arrays["masks"] = np.ascontiguousarray(
        np.where(masks, 0.0, -1e30).transpose(2, 0, 1, 3).astype(ml_dtypes.bfloat16))
    sels = np.zeros((128, 384), np.float32)
    sels[0, 0:128] = 1.0
    sels[1, 128:256] = 1.0
    sels[:, 256:384] = np.eye(128)
    arrays["sels"] = sels

    nc = bacc.Bacc("TRN2", target_bir_lowering=False, num_devices=1)
    aps = {k: nc.dram_tensor(k, v.shape, mybir.dt.from_np(v.dtype), kind="ExternalInput").ap()
           for k, v in arrays.items()}
    out = nc.dram_tensor("out", (BATCH, T, D), F32, kind="ExternalOutput").ap()
    build(nc, out=out, **aps)
    return run(nc, [arrays], core_ids=[0]).results[0]["out"]
```

```python
import concourse.bass as bass
from concourse import mybir
from contextlib import ExitStack

F32 = mybir.dt.float32
F32R = mybir.dt.float32r
BF16 = mybir.dt.bfloat16
ALU = mybir.AluOpType
ACT = mybir.ActivationFunctionType
AX = mybir.AxisListType

BATCH, T, D = 2, 1024, 256
HEADS, KV, DH = 16, 4, 128
G = HEADS // KV
WINDOW = 64
HID, K_STEPS = 1024, 4
TILES = BATCH * T // 128
STEPS = TILES * KV
DC = D // 128
HC = HID // 128
REP = 512 // HC // 2
TPB = T // 128
PAIRS = TILES // 2
EPS_X, EPS_N, EPS_R = 1e-5, 1e-6, 1e-6
Q_P, Q_K, Q_V, Q_G, JOBS = (0, 2, 4, 6), 1, 3, 5, 7


def build(nc, x, wq, wk, wv, wo, gw, aggw, d1w, d2w, bcw, cols, bcrow, rows128, gbrow, rope, masks, ident, out):
    ctx = ExitStack()
    with ctx:
        def sb(name, shape, dt=F32):
            return ctx.enter_context(nc.sbuf_tensor(name, shape, dt))

        def pb(name, shape=(128, 512)):
            return ctx.enter_context(nc.psum_tensor(name, list(shape), F32))

        def sem(name):
            return ctx.enter_context(nc.semaphore(name))

        Wq = sb("Wq", [128, 2, KV, DC, 512], F32R)
        Wk = sb("Wk", [128, 2, DC, 512], F32R)
        Wv = sb("Wv", [128, 2, DC, 512], F32R)
        Wo = sb("Wo", [128, 2, HEADS, D], F32R)
        Wg = sb("Wg", [128, 2, DC, D], F32R)
        gb_part = sb("gb_part", [128, D], F32R)
        gb_sel = sb("gb_sel", [128, 128], F32R)
        store = sb("store", [128, 4 * 1024])
        t1 = [store[:, 512 * k:512 * k + 512] for k in (0, 1)]
        t2 = [store[:, 512 * k:512 * k + 512] for k in (2, 3)]
        qT = [store[:, 512 * k:512 * k + 512] for k in (4, 5)]
        prob = [store[:, 512 * k:512 * k + 512] for k in (6, 7)]
        cosq, sinq, cosk, sink = (sb(f"rope{k}", [128, TPB, DH]) for k in range(4))
        bc128 = sb("bc128", [128, 2 * D + 2 * DH])
        out_gamma, out_beta = bc128[:, 0:D], bc128[:, D:2 * D]
        maskt = sb("maskt", [128, 4, 2, 128], BF16)
        identf = sb("identf", [128, 128])
        identb = sb("identb", [128, 128], BF16)
        neghalf, eps_x, eps_n, eps_r = (sb(n, [128, 4]) for n in ("neghalf", "eps_x", "eps_n", "eps_r"))
        hb = sb("hb", [128, BATCH, D])
        d1_s = sb("d1_s", [128, DC, HID])
        d2_s = sb("d2_s", [128, HC, D])
        colv = sb("colv", [128, HC + 8 * DC])
        mean_w = sb("mean_w", [128, 128])
        f_cent, f_sq, f_sc, f_t, th, thb = (sb(n, [128, DC, 2]) for n in ("f_cent", "f_sq", "f_sc", "f_t", "th", "thb"))
        fve = sb("fve", [128, 2])
        frs = sb("frs", [128, 2])
        zz = sb("zz", [128, HC, 2])
        hT = sb("hT", [128, HC, 2])
        late = sb("late", [128, 8 * D])
        gth, gu, gz, gsl, gy, so, gg = (late[:, D * k:D * k + D] for k in range(7))
        agg_s = late[:, 0:DC * D].rearrange("p (c d) -> p c d", c=DC)
        bc_s = late[:, DC * D:2 * DC * D].rearrange("p (c d) -> p c d", c=DC)
        thB = late[:, 4 * D:6 * D].rearrange("p (b c t) -> p b c t", b=BATCH, c=DC)
        gbh = late[0:64, 6 * D:7 * D].bitcast(F32R)
        bcb = late[:, 7 * D:8 * D]
        xt = [sb(f"xt{k}", [128, D]) for k in (0, 1)]
        xr = [sb(f"xr{k}", [128, D]) for k in (0, 1)]
        xn = [sb(f"xn{k}", [128, D]) for k in (0, 1)]
        xT = [sb(f"xT{k}", [128, 2, DC, 128], F32R) for k in (0, 1)]
        kTb = [sb(f"kT{k}", [128, KV, 192]) for k in (0, 1)]
        Va = [sb(f"Va{k}", [128, 2, 512], F32R) for k in (0, 1)]
        Vb = [sb(f"Vb{k}", [128, 2, 512], F32R) for k in (0, 1)]
        kt = sb("kt", [128, 2 * 512])
        kt1, kt2 = kt[:, 0:512], kt[:, 512:1024]
        gbr = xr[0][0:64, :]
        kss = sb("kss", [128, KV])
        kr = sb("kr", [128, KV])
        kr2 = sb("kr2", [128, KV])
        junkk = sb("junkk", [128, 512], BF16)
        lst = sb("lst", [128, 6])
        lmv = sb("lmv", [128, 2])
        lve = sb("lve", [128, 1])
        lrs = sb("lrs", [128, 1])
        gst = sb("gst", [128, 6])
        gmv = sb("gmv", [128, 2])
        gve = sb("gve", [128, 1])
        grs = sb("grs", [128, 1])
        junk = sb("junk", [128, 512], BF16)
        ss = [sb(f"ss{k}", [128, G]) for k in (0, 1)]
        sse = [sb(f"sse{k}", [128, G]) for k in (0, 1)]
        rq = [sb(f"rq{k}", [128, G]) for k in (0, 1)]
        r2 = [sb(f"r2{k}", [128, 2, 2]) for k in (0, 1)]
        nmx = [sb(f"nmx{k}", [128, 4]) for k in (0, 1)]
        nb = [sb(f"nb{k}", [128, 4]) for k in (0, 1)]
        rsum = [sb(f"rsum{k}", [128, 4]) for k in (0, 1)]
        rinv = [sb(f"rinv{k}", [128, 4]) for k in (0, 1)]
        pT = [sb(f"pT{k}", [128, 2, 2, 2, 128], F32R) for k in (0, 1)]
        cT = [sb(f"cT{k}", [128, 2, G, 2, 64], F32R) for k in (0, 1)]

        PA = [pb("pa0"), pb("pa1")]
        TR = [pb("tr0"), pb("tr1")]
        SC = [pb("sc0"), pb("sc1")]
        CT = pb("ct")
        OU = pb("ou")
        F_MEAN, F_VAR = OU[:, 0:2], OU[:, 2:4]
        f_out = OU[:, :].rearrange("p (m r b) -> p m r b", r=REP, b=2)
        F_D1, F_TH = f_out[:, 0:HC, 0, :], f_out[:, 0:DC, 0, :]
        d1_b = colv[:, 0:HC]
        in_gamma, in_beta, pn_gamma, pn_beta, agg_b, d2_b = (
            colv[:, HC + DC * k:HC + DC * k + DC].unsqueeze(2).to_broadcast([128, DC, 2]) for k in range(6))
        x_last = colv[:, HC + 6 * DC:HC + 8 * DC].rearrange("p (c b) -> p c b", b=2)

        l_b128, l_gb, l_mask, l_ident, l_cols, l_agg, l_d1, l_d2, l_bc, l_bcb = (
            sem(n) for n in ("l_b128", "l_gb", "l_mask", "l_ident", "l_cols", "l_agg", "l_d1", "l_d2", "l_bc", "l_bcb"))
        l_x = [sem("l_x0"), sem("l_x1")]
        l_xr = [sem("l_xr0"), sem("l_xr1")]
        l_vlow = [sem("l_vlow0"), sem("l_vlow1")]
        l_vup = [sem("l_vup0"), sem("l_vup1")]
        st_out = [sem("st_out0"), sem("st_out1")]
        a_whi, d_wlo, p_init, d_tab, d_one = (sem(n) for n in ("a_whi", "d_wlo", "p_init", "d_tab", "d_one"))
        f_dve, f_act, f_pe, f_pool = sem("f_dve"), sem("f_act"), sem("f_pe"), sem("f_pool")
        f_link, f_ve, f_gam, f_thb = sem("f_link"), sem("f_ve"), sem("f_gam"), sem("f_thb")
        pe_xT, pe_pa, pe_T, pe_kT, pe_S, pe_X, pe_C, pe_O = (
            sem(n) for n in ("pe_xT", "pe_pa", "pe_T", "pe_kT", "pe_S", "pe_X", "pe_C", "pe_O"))
        a_xhi, a_qT, a_ssq, a_kss, a_vhi, a_kT, a_pt, a_exp, a_ct, a_gate, a_silu = (
            sem(n) for n in ("a_xhi", "a_qT", "a_ssq", "a_kss", "a_vhi", "a_kT", "a_pt", "a_exp", "a_ct",
                             "a_gate", "a_silu"))
        d_lst, d_lmv, d_xn, d_xlo, d_rope, d_krope, d_kadd, d_vlo, d_r2, d_mx, d_nb, d_pt, d_ct, d_rinv = (
            sem(n) for n in ("d_lst", "d_lmv", "d_xn", "d_xlo", "d_rope", "d_krope", "d_kadd", "d_vlo", "d_r2", "d_mx",
                             "d_nb", "d_pt", "d_ct", "d_rinv"))
        d_gu, d_gst, d_gmv, d_g1, d_g2, d_gg, d_out = (
            sem(n) for n in ("d_gu", "d_gst", "d_gmv", "d_g1", "d_g2", "d_gg", "d_out"))
        p_lve, p_lrs, p_add, p_sse, p_r, p_norm, p_kve, p_kr, p_k, p_gy, p_gve, p_grs, p_fin = (
            sem(n) for n in ("p_lve", "p_lrs", "p_add", "p_sse", "p_r", "p_norm", "p_kve", "p_kr",
                             "p_k", "p_gy", "p_gve", "p_grs", "p_fin"))

        quarter = [store[:, 1024 * k:1024 * k + 1024] for k in range(4)] + [kt[:, :]]

        def wq_parts(g):
            return wq[:, g], Wq[:, 0, g], Wq[:, 1, g]

        def wo_parts(g):
            return wo[:, G * g:G * g + G], Wo[:, 0, G * g:G * g + G], Wo[:, 1, G * g:G * g + G]

        chunks = [(*wq_parts(0), quarter[0]), (wk, Wk[:, 0], Wk[:, 1], quarter[1]),
                  (wv, Wv[:, 0], Wv[:, 1], quarter[4]),
                  (*wq_parts(1), quarter[0]), (*wq_parts(2), quarter[1]), (*wq_parts(3), quarter[2]),
                  (gw, Wg[:, 0], Wg[:, 1], quarter[3]),
                  (*wo_parts(0), quarter[4]), (*wo_parts(1), quarter[0]), (*wo_parts(2), quarter[1]),
                  (*wo_parts(3), quarter[2])]
        W_Q, W_K, W_V, W_G, W_O = (0, 3, 4, 5), 1, 2, 6, (7, 8, 9, 10)
        NW = len(chunks)
        l_w = [sem(f"l_w{k}") for k in range(NW)]
        l_cos, l_sin = sem("l_cos"), sem("l_sin")

        def staged(k):
            src, hi, _, place = chunks[k]
            return place[:, 0:hi.shape[1] * hi.shape[2]].rearrange("p (a b) -> p a b", b=hi.shape[2])

        block = ctx.enter_context(nc.Block())

        def exists(s, lag=0):
            return not isinstance(s, int) or 0 <= s - lag < STEPS

        def tile_exists(n):
            return not isinstance(n, int) or 0 <= n < TILES

        def later(n, least=1):
            return not isinstance(n, int) or n >= least

        def wait(eng, s, n):
            if later(n):
                eng.wait_ge(s, n)

        def program(engine, slot):
            for k in range(8):
                slot(0, k, k)
            with engine.Fori(1, PAIRS - 1) as i:
                for k in range(8):
                    slot(i, k, 8 * i + k)
            for k in range(8 + 8):
                slot(PAIRS - 1 + k // 8, k % 8, 8 * (PAIRS - 1) + k)

        @block.sync
        def _(sp):
            sp.dma_start(colv[:, :], cols).then_inc(l_cols, 16)
            sp.dma_start(xt[0][:, :], x[0, 0:128, :]).then_inc(l_x[0], 16)
            sp.dma_start(identf[:, :], ident).then_inc(l_ident, 16)
            sp.dma_start(agg_s[:, :, :], aggw).then_inc(l_agg, 16)

            def load_w(k):
                sp.dma_start(staged(k), chunks[k][0]).then_inc(l_w[k], 16)

            sp.dma_start(d1_s[:, :, :], d1w).then_inc(l_d1, 16)
            load_w(0)
            sp.dma_start(d2_s[:, :, :], d2w).then_inc(l_d2, 16)
            sp.dma_start(bc128[:, :], rows128.partition_broadcast(128)).then_inc(l_b128, 16)
            for k, sem_r in ((0, l_cos), (1, l_sin)):
                sp.dma_start(quarter[2 + k].rearrange("p (m d) -> p m d", d=DH), rope[:, k, :, :]).then_inc(sem_r, 16)
            load_w(1)
            sp.dma_start(xt[1][:, :], x[0, 128:256, :]).then_inc(l_x[1], 16)
            sp.dma_start(gbr[0:1, :], gbrow).then_inc(l_gb, 16)
            sp.dma_start(gbr[32:33, :], gbrow).then_inc(l_gb, 16)
            load_w(2)
            sp.dma_start(maskt[:, 0:2, :, :], masks).then_inc(l_mask, 16)
            for k, before in ((3, 0), (4, 1), (5, None), (6, None), (7, 2), (8, 3), (9, 4), (10, 5)):
                if before is None:
                    sp.wait_ge(d_tab, 1)
                else:
                    sp.wait_ge(a_whi, before + 1)
                    sp.wait_ge(d_wlo, before + 1)
                load_w(k)
            sp.dma_start(bc_s[:, :, :], bcw).then_inc(l_bc, 16)
            sp.dma_start(bcb, bcrow.partition_broadcast(128)).then_inc(l_bcb, 16)

            def slot(i, k, s):
                par, j, n = k // 4, k % 4, 2 * i + k // 4
                own = isinstance(i, int)
                if j == 0 and tile_exists(n) and (not own or n + 2 < TILES):
                    sp.wait_ge(d_xn, n + 1)
                    nxt = n + 2
                    sp.dma_start(xt[par][:, :], x.rearrange("b t d -> (b t) d")[bass.ds(nxt * 128, 128), :])\
                        .then_inc(l_x[par], 16)
                if j == 2 and tile_exists(n):
                    sp.wait_ge(d_vlo, n + 1)
                    wait(sp, pe_C, 4 * n - 4)
                    sp.dma_start(Vb[par][0:64, :, :].bitcast(F32), Va[par][0:64, :, :].bitcast(F32)).then_inc(l_vlow[par], 16)
                if j == 3 and tile_exists(n):
                    wait(sp, pe_C, 4 * n)
                    sp.wait_ge(d_vlo, n + 1)
                    sp.dma_start(Vb[1 - par][64:128, :, :].bitcast(F32), Va[par][64:128, :, :].bitcast(F32)).then_inc(l_vup[par], 16)
                if j == 3 and (not own or n >= 2):
                    sp.wait_ge(p_fin, n - 1)
                    prev = n - 2
                    sp.dma_start(out.rearrange("b t d -> (b t) d")[bass.ds(prev * 128, 128), :], xr[par][:, :])\
                        .then_inc(st_out[par], 16)
                if j == 3 and tile_exists(n):
                    if later(n, 2):
                        sp.wait_ge(st_out[par], 16 * i)
                    sp.dma_start(xr[par][:, :], x.rearrange("b t d -> (b t) d")[bass.ds(n * 128, 128), :])\
                        .then_inc(l_xr[par], 16)
            program(nc.sync, slot)
            for par in (0, 1):
                sp.wait_ge(l_vup[par], 16 * PAIRS)
                sp.wait_ge(st_out[par], 16 * PAIRS)

        @block.tensor
        def _(pe):

            def f_mean(dst, src, ready):
                pe.wait_ge(f_dve, ready)
                for c in range(DC):
                    last = nc.tensor.matmul(dst, mean_w[:, :], src[:, c, :], start=(c == 0), stop=(c == DC - 1))
                last.then_inc(f_pe, 1)

            def f_product(w, src, n_in, n_out):
                for m in range(n_out):
                    for c in range(n_in):
                        last = nc.tensor.matmul(f_out[:, m], w[:, c, 128 * m:128 * m + 128],
                                                src[:, c, :].unsqueeze(1).to_broadcast([128, REP, 2]),
                                                start=(c == 0), stop=(c == n_in - 1))
                last.then_inc(f_pe, 1)

            def step_mean(k):
                f_mean(F_MEAN, th, 5 + 4 * k)

            def step_var(k):
                f_mean(F_VAR, f_sq, 6 + 4 * k)

            def step_d1(k):
                pe.wait_ge(l_d1, 16)
                pe.wait_ge(f_dve, 7 + 4 * k)
                f_product(d1_s, f_t, DC, HC)

            def step_d2(k):
                pe.wait_ge(l_d2, 16)
                pe.wait_ge(f_act, k + 1)
                f_product(d2_s, hT, HC, DC)

            def broadcast_rows():
                pe.wait_ge(l_bc, 16)
                pe.wait_ge(f_dve, 6 + 4 * K_STEPS)
                for b in range(BATCH):
                    for c in range(DC):
                        last = nc.tensor.matmul(OU[:, D * b:D * b + D], thB[:, b, c, :], bc_s[:, c, :],
                                                start=(c == 0), stop=(c == DC - 1))
                last.then_inc(f_pe, 1)

            def x_turn(n, par):
                pe.wait_ge(d_xn, n + 1)
                for c in range(DC):
                    last = nc.tensor.transpose(TR[1][:, 128 * c:128 * c + 128], xn[par][:, 128 * c:128 * c + 128],
                                               identf[:, :])
                last.then_inc(pe_xT, 1)

            def product(dst, par, w, start):
                for c in range(DC):
                    for p, q in ((0, 0), (0, 1), (1, 0)):
                        last = nc.tensor.matmul(dst, xT[par][:, p, c, :], w[:, q, c, :],
                                                start=(start and c == 0 and p + q == 0),
                                                stop=(c == DC - 1 and p == 1))
                last.then_inc(pe_pa, 1)

            pe.wait_ge(p_init, 5)
            pe.wait_ge(l_cols, 16)
            for c in range(DC):
                last = nc.tensor.matmul(F_MEAN, mean_w[:, :], x_last[:, c, :], start=(c == 0), stop=(c == DC - 1))
            last.then_inc(f_pe, 1)
            f_mean(F_VAR, f_sq, 1)
            f_mean(F_MEAN, th, 2)
            f_mean(F_VAR, f_sq, 3)
            pe.wait_ge(l_agg, 16)
            pe.wait_ge(f_dve, 4)
            f_product(agg_s, f_t, DC, DC)
            pe.wait_ge(l_ident, 16)
            x_turn(0, 0)
            step_mean(0)
            step_var(0)
            step_d1(0)
            step_d2(0)

            def slot(i, k, s):
                par, j, n = k // 4, k % 4, 2 * i + k // 4
                tr = {0: (0, 1), 1: (0, 1), 2: (0, 0), 3: (1, 0)}[j]
                first = isinstance(i, int) and i == 0
                if exists(s, 2):
                    t = s - 2
                    pe.wait_ge(p_add, t + 1)
                    if j == 0:
                        wait(pe, d_pt, t - 1)
                    if j in (1, 2):
                        wait(pe, a_qT, t)
                    if j == 3:
                        pe.wait_ge(a_kT, n + 1)
                    turned = TR[tr[0]][:, :].rearrange("p (a u e t) -> p a e u t", a=2, u=2, e=2)
                    for h in range(G):
                        last = nc.tensor.transpose(turned[:, h // 2, h % 2],
                                                   t1[(k - 2) % 2][:, 128 * h:128 * h + 128], identf[:, :])
                    last.then_inc(pe_T, 1)
                if first and s in (2, 3):
                    step_mean(s)
                if j == 2 and tile_exists(n):
                    pe.wait_ge(p_k, n + 1)
                    wait(pe, d_pt, 4 * n - 1)
                    for h in range(KV):
                        last = nc.tensor.transpose(TR[1][:, 128 * h:128 * h + 128], kt1[:, 128 * h:128 * h + 128],
                                                   identf[:, :])
                    last.then_inc(pe_kT, 1)
                if first and s == 2:
                    step_var(2)
                if first and s == 4:
                    broadcast_rows()
                if exists(s, 5):
                    t = s - 5
                    jt, pt = (k - 5) % 4, ((k - 5) // 4) % 2
                    pe.wait_ge(d_ct, t + 1)
                    if jt == 0:
                        wait(pe, d_out, n - 1)
                    if isinstance(t, int) and t < KV:
                        pe.wait_ge(d_wlo, W_O[jt] + 1)
                    for h in range(G):
                        for p, q in ((0, 0), (0, 1), (1, 0)):
                            last = nc.tensor.matmul(OU[:, 0:D],
                                                    cT[(k - 5) % 2][:, p, h, :, :].rearrange("p u t -> p (u t)"),
                                                    Wo[:, q, G * jt + h, :],
                                                    start=(jt == 0 and h == 0 and p + q == 0),
                                                    stop=(jt == KV - 1 and h == G - 1 and p == 1))
                    last.then_inc(pe_O, 1)
                if exists(s, 2):
                    t = s - 2
                    jt, pt = (k - 2) % 4, ((k - 2) // 4) % 2
                    nt = n if j >= 2 else n - 1
                    it = i if k >= 2 else i - 1
                    pe.wait_ge(a_qT, t + 1)
                    pe.wait_ge(a_kT, nt + 1)
                    wait(pe, a_exp, t - 1)
                    if first:
                        pe.wait_ge(p_init, 6)
                        pe.wait_ge(d_one, 4)
                        pe.wait_ge(l_mask, 16)
                    bank = SC[k % 2]
                    if pt == 0:
                        mk = maskt[:, bass.ds(it % 4, 1), :, :]
                    else:
                        mk = maskt[:, 1:2, :, :]
                    nc.tensor.matmul(bank[:, :].rearrange("p (a u c) -> p a u c", a=2, u=2), identb[:, :],
                                     mk.to_broadcast([128, 2, 2, 128]), start=True, stop=False)
                    keys = kTb[pt][:, jt, :].rearrange("p (a c) -> p a c", c=64)
                    for p in range(2):
                        for u in range(2):
                            at = 128 * (2 * p + u)
                            kk = keys[:, 0:2, :] if u else keys[:, 0:3:2, :]
                            last = nc.tensor.matmul(bank[:, at:at + 128].rearrange("p (a c) -> p a c", a=2),
                                                    qT[k % 2][:, at:at + 128], kk, start=False,
                                                    stop=(p == 1 and u == 1))
                    last.then_inc(pe_S, 1)
                if exists(s, 3):
                    t = s - 3
                    pe.wait_ge(p_norm, t + 1)
                    if j == 0 and tile_exists(n):
                        pe.wait_ge(d_xlo, n + 1)
                    if j == 2 and tile_exists(n):
                        pe.wait_ge(a_qT, t + 2)
                    if j in (0, 2) and not tile_exists(n):
                        pe.wait_ge(a_qT, t + 1)
                    if j in (1, 3):
                        wait(pe, d_pt, t)
                    for c in range(4):
                        last = nc.tensor.transpose(TR[tr[1]][:, 128 * c:128 * c + 128],
                                                   prob[(k - 3) % 2][:, 128 * c:128 * c + 128], identf[:, :])
                    last.then_inc(pe_X, 1)
                if first and s == 3:
                    step_var(3)
                if exists(s):
                    if first:
                        pe.wait_ge(d_wlo, W_Q[j] + 1)
                    if j == 0:
                        pe.wait_ge(d_xlo, n + 1)
                        wait(pe, a_gate, n)
                    else:
                        pe.wait_ge(a_ssq, s)
                    product(PA[(par + Q_P[j]) % 2][:, :], par, Wq[:, :, j], True)
                if first and s == 0:
                    step_mean(1)
                if first and s in (1, 2, 3):
                    step_d1(s)
                if tile_exists(n):
                    if j == 0:
                        if first:
                            pe.wait_ge(d_wlo, W_K + 1)
                        wait(pe, a_ssq, 4 * n)
                        product(PA[(par + Q_K) % 2][:, :], par, Wk, True)
                    if j == 1:
                        if first:
                            pe.wait_ge(d_wlo, W_V + 1)
                        pe.wait_ge(a_kss, n + 1)
                        product(PA[(par + Q_V) % 2][:, :], par, Wv, True)
                    if j == 2:
                        if first:
                            pe.wait_ge(d_wlo, W_G + 1)
                            pe.wait_ge(d_one, 4)
                        pe.wait_ge(d_vlo, n + 1)
                        dst = PA[(par + Q_G) % 2][:, 0:D]
                        nc.tensor.matmul(dst, gb_sel[:, :], gb_part[:, :], start=True, stop=False)
                        product(dst, par, Wg, False)
                if j == 3 and tile_exists(n + 1):
                    pe.wait_ge(a_qT, 4 * n + 2)
                    x_turn(n + 1, 1 - par)
                if first and s == 0:
                    step_var(1)
                if first and s in (1, 2, 3):
                    step_d2(s)
                if exists(s, 3):
                    t = s - 3
                    jt, pt = (k - 3) % 4, ((k - 3) // 4) % 2
                    pe.wait_ge(d_pt, t + 1)
                    it = i if k >= 3 else i - 1
                    pe.wait_ge(l_vlow[pt], 16 * (it + 1))
                    wait(pe, l_vup[1 - pt], 16 * (it + pt))
                    wait(pe, d_ct, t)
                    for u in range(2):
                        V = (Vb, Va)[u][pt]
                        for p, q in ((0, 0), (0, 1), (1, 0)):
                            last = nc.tensor.matmul(
                                CT[:, 256 * u:256 * u + 256].rearrange("p (a c) -> p a c", a=2),
                                V[:, p, DH * jt:DH * jt + DH], pT[(k - 3) % 2][:, q, :, u, :],
                                start=(p + q == 0), stop=(p == 1))
                    last.then_inc(pe_C, 1)
            program(nc.tensor, slot)

        @block.scalar
        def _(act):
            def w_hi(k):
                act.wait_ge(l_w[k], 16)
                nc.scalar.activation(chunks[k][1], staged(k), ACT.Identity).then_inc(a_whi, 1)

            def x_hi(n, par):
                nc.scalar.activation(xT[par][:, 0, :, :], TR[1][:, 0:D].rearrange("p (c t) -> p c t", c=DC),
                                     ACT.Identity).then_inc(a_xhi, 1)

            def gelu(k):
                act.wait_ge(f_dve, 8 + 4 * k)
                nc.scalar.activation(hT[:, :, :], zz[:, :, :], ACT.Gelu).then_inc(f_act, 1)

            w_hi(0)
            w_hi(1)
            gelu(0)
            for c in range(2, 4):
                w_hi(c)

            def slot(i, k, s):
                par, j, n = k // 4, k % 4, 2 * i + k // 4
                if j == 0 and tile_exists(n):
                    act.wait_ge(pe_xT, n + 1)
                    x_hi(n, par)
                if isinstance(s, int) and s == 0:
                    for c in range(4, NW):
                        w_hi(c)
                if exists(s, 2):
                    t = s - 2
                    act.wait_ge(pe_T, t + 1)
                    wait(act, pe_S, t - 1)
                    nc.scalar.activation(qT[k % 2], TR[1 if j == 3 else 0][:, :], ACT.Identity).then_inc(a_qT, 1)
                if j == 2 and tile_exists(n):
                    act.wait_ge(pe_kT, n + 1)
                    src = TR[1][:, :].rearrange("p (h t) -> p h t", h=KV)
                    nc.scalar.activation(kTb[par][:, :, 0:128], src, ACT.Identity)
                    nc.scalar.activation(kTb[1 - par][:, :, 128:192], src[:, :, 64:128], ACT.Identity).then_inc(a_kT, 1)
                if exists(s, 4):
                    t = s - 4
                    act.wait_ge(pe_C, t + 1)
                    wait(act, pe_O, t - 1)
                    nc.scalar.activation(cT[k % 2][:, 0].rearrange("p h u t -> p u h t"),
                                         CT[:, :].rearrange("p (u h t) -> p u h t", u=2, h=G),
                                         ACT.Identity).then_inc(a_ct, 1)
                if exists(s, 1):
                    t = s - 1
                    jt, pt = (k - 1) % 4, ((k - 1) // 4) % 2
                    act.wait_ge(d_rope, t + 1)
                    wait(act, p_sse, t - 1)
                    wait(act, a_ssq, t)
                    for h in range(G):
                        last = nc.scalar.activation(junk[:, 128 * h:128 * h + 128],
                                                    PA[(pt + Q_P[jt]) % 2][:, 128 * h:128 * h + 128], ACT.Square,
                                                    accum_out=ss[(k - 1) % 2][:, h:h + 1])
                    last.then_inc(a_ssq, 1)
                if j == 1 and tile_exists(n):
                    act.wait_ge(d_krope, n + 1)
                    wait(act, p_kve, n)
                    wait(act, a_kss, n)
                    for h in range(KV):
                        last = nc.scalar.activation(junkk[:, 128 * h:128 * h + 128],
                                                    PA[(par + Q_K) % 2][:, 128 * h:128 * h + 128], ACT.Square,
                                                    accum_out=kss[:, h:h + 1])
                    last.then_inc(a_kss, 1)
                if j == 2 and tile_exists(n):
                    act.wait_ge(pe_pa, JOBS * n + Q_V + 1)
                    wait(act, l_vlow[par], 16 * i)
                    wait(act, l_vup[par], 16 * i)
                    wait(act, pe_C, 4 * n - 4)
                    nc.scalar.activation(Va[par][:, 0, :], PA[(par + Q_V) % 2][:, :], ACT.Identity).then_inc(a_vhi, 1)
                if j == 3 and tile_exists(n):
                    act.wait_ge(pe_pa, JOBS * n + Q_G + 1)
                    wait(act, d_gu, n)
                    nc.scalar.activation(gth[:, :], PA[(par + Q_G) % 2][:, 0:D], ACT.Tanh, scale=0.5).then_inc(a_gate, 1)
                if exists(s, 3):
                    t = s - 3
                    act.wait_ge(pe_X, t + 1)
                    wait(act, pe_C, t - 1)
                    nc.scalar.activation(pT[(k - 3) % 2][:, 0],
                                         TR[0 if j >= 2 else 1][:, :].rearrange("p (a u c) -> p a u c", a=2, u=2),
                                         ACT.Identity).then_inc(a_pt, 1)
                if exists(s, 2):
                    t = s - 2
                    act.wait_ge(d_nb, t + 1)
                    wait(act, pe_X, t - 1)
                    for c in range(4):
                        last = nc.scalar.activation(prob[k % 2][:, 128 * c:128 * c + 128],
                                                    SC[k % 2][:, 128 * c:128 * c + 128], ACT.Exp,
                                                    bias=nb[k % 2][:, c:c + 1], scale=r2[k % 2][:, c // 2, c % 2:c % 2 + 1],
                                                    accum_out=rsum[k % 2][:, c:c + 1])
                    last.then_inc(a_exp, 1)
                if j == 3 and tile_exists(n - 1):
                    act.wait_ge(d_g2, n)
                    wait(act, d_gg, n - 1)
                    nc.scalar.activation(gsl[:, :], gz[:, :], ACT.Tanh, scale=0.5).then_inc(a_silu, 1)
                if isinstance(s, int) and s in (1, 2, 3):
                    gelu(s)
            program(nc.scalar, slot)

        @block.gpsimd
        def _(pool):
            def rsqrt(dst, tmp, src, eps, s_tmp, n_tmp, s_dst):
                p, w = tmp.shape[0], tmp.shape[-1]
                nc.gpsimd.tensor_tensor(tmp, src, eps[0:p, 0:w], ALU.add).then_inc(s_tmp, 1)
                pool.wait_ge(s_tmp, n_tmp)
                nc.gpsimd.tensor_tensor(dst, tmp, neghalf[0:p, 0:w], ALU.pow).then_inc(s_dst, 1)

            nc.gpsimd.memset(eps_x[:, :], EPS_X)
            nc.gpsimd.memset(eps_n[:, :], EPS_N)
            nc.gpsimd.memset(eps_r[:, :], DH * EPS_R)
            nc.gpsimd.memset(neghalf[:, :], -0.5).then_inc(p_init, 1)
            nc.gpsimd.memset(kTb[0][:, :, 128:192], 0.0).then_inc(p_init, 1)
            nc.gpsimd.memset(Vb[0][:, :, :].bitcast(F32), 0.0).then_inc(p_init, 1)
            nc.gpsimd.memset(gb_part[:, :].bitcast(F32), 0.0).then_inc(p_init, 1)
            nc.gpsimd.memset(gb_sel[:, :].bitcast(F32), 0.0)
            nc.gpsimd.memset(mean_w[:, :], 1.0 / D).then_inc(p_init, 1)
            pool.wait_ge(p_init, 5)
            pool.wait_ge(d_lmv, 1)
            rsqrt(lrs[:, :], lve[:, :], lmv[:, 1:2], eps_x, p_lve, 1, p_lrs)

            def f_root(m):
                pool.wait_ge(f_ve, m + 1)
                nc.gpsimd.tensor_tensor(frs[:, :], fve[:, :], neghalf[:, 0:2], ALU.pow).then_inc(f_pool, 1)

            for m in range(3):
                f_root(m)
            pool.wait_ge(l_mask, 16)
            nc.gpsimd.tensor_copy(maskt[:, 2:4, :, :], maskt[:, 1:2, :, :].to_broadcast([128, 2, 2, 128]))\
                .then_inc(p_init, 1)

            def slot(i, k, s):
                par, j, n = k // 4, k % 4, 2 * i + k // 4
                if exists(s, 3):
                    t = s - 3
                    pool.wait_ge(d_rinv, t + 1)
                    p3 = prob[(k - 3) % 2].rearrange("p (c n) -> p c n", c=4)
                    nc.gpsimd.tensor_tensor(p3, p3, rinv[(k - 3) % 2][:, :].unsqueeze(2).to_broadcast([128, 4, 128]),
                                            ALU.mult).then_inc(p_norm, 1)
                if exists(s, 1):
                    t = s - 1
                    q = (k - 1) % 2
                    pool.wait_ge(d_rope, t + 1)
                    nc.gpsimd.tensor_tensor(t1[q], t1[q], t2[q], ALU.add).then_inc(p_add, 1)
                if isinstance(s, int) and s == 2:
                    f_root(4)
                if exists(s, 1):
                    pool.wait_ge(a_ssq, t + 1)
                    wait(pool, d_r2, t - 1)
                    rsqrt(rq[q][:, :], sse[q][:, :], ss[q][:, :], eps_r, p_sse, t + 1, p_r)
                if j == 0 and tile_exists(n - 1):
                    pool.wait_ge(d_gu, n)
                    wait(pool, d_g1, n - 1)
                    nc.gpsimd.tensor_tensor(gy[:, :], gu[:, :], xn[1 - par][:, :], ALU.add).then_inc(p_gy, 1)
                if isinstance(s, int) and s == 0:
                    f_root(3)
                if j == 0 and tile_exists(n + 1):
                    pool.wait_ge(d_lmv, n + 2)
                    rsqrt(lrs[:, :], lve[:, :], lmv[:, 1:2], eps_x, p_lve, n + 2, p_lrs)
                if j == 1 and tile_exists(n):
                    pool.wait_ge(a_kss, n + 1)
                    rsqrt(kr2[:, :], kr[:, :], kss[:, :], eps_r, p_kve, n + 1, p_kr)
                    pool.wait_ge(d_kadd, n + 1)
                    pool.wait_ge(p_kr, n + 1)
                    k3 = kt1[:, :].rearrange("p (h d) -> p h d", h=KV)
                    nc.gpsimd.tensor_tensor(k3, k3, kr2[:, :].unsqueeze(2).to_broadcast([128, KV, DH]),
                                            ALU.mult).then_inc(p_k, 1)
                if j == 2 and tile_exists(n - 1):
                    pool.wait_ge(d_gmv, n)
                    rsqrt(grs[:, :], gve[:, :], gmv[:, 1:2], eps_n, p_gve, n, p_grs)
                if j == 3 and (not isinstance(n, int) or n >= 2):
                    pool.wait_ge(d_out, n - 1)
                    pool.wait_ge(l_xr[par], 16 * i)
                    nc.gpsimd.tensor_tensor(xr[par][:, :], so[:, :], xr[par][:, :], ALU.add).then_inc(p_fin, 1)
                if isinstance(s, int) and s == 3:
                    f_root(5)
            program(nc.gpsimd, slot)

        @block.vector
        def _(dve):
            chain = [0]

            def link(ins):
                chain[0] += 1
                ins.then_inc(f_link, 1)
                dve.wait_ge(f_link, chain[0])

            def w_lo(k):
                dve.wait_ge(a_whi, k + 1)
                _, hi, lo, _ = chunks[k]
                nc.vector.tensor_tensor(lo, staged(k), hi.bitcast(F32), ALU.subtract).then_inc(d_wlo, 1)

            def x_lo(n, par):
                dve.wait_ge(a_xhi, n + 1)
                nc.vector.tensor_tensor(xT[par][:, 1, :, :], TR[1][:, 0:D].rearrange("p (c t) -> p c t", c=DC),
                                        xT[par][:, 0, :, :].bitcast(F32), ALU.subtract).then_inc(d_xlo, 1)

            def x_stats(n, par):
                nc.vector.bn_stats(lst[:, :], xt[par][:, :]).then_inc(d_lst, 1)
                dve.wait_ge(l_x[0], 16)
                dve.wait_ge(d_lst, n)
                nc.vector.bn_aggr(lmv[:, :], lst[:, :]).then_inc(d_lmv, 1)

            def x_norm(n, par):
                dve.wait_ge(p_lrs, n + 1)
                dve.wait_ge(d_lmv, n + 1)
                nc.vector.tensor_scalar(xn[par][:, :], xt[par][:, :], lmv[:, 0:1], lrs[:, 0:1], ALU.subtract,
                                        ALU.mult).then_inc(d_xn, 1)

            def over_rows(v):
                return v.unsqueeze(1).to_broadcast([128, DC, 2])

            def f_center(src, n_pe):
                dve.wait_ge(f_pe, n_pe)
                link(nc.vector.tensor_tensor(f_cent[:, :, :], src, over_rows(F_MEAN), ALU.subtract))
                nc.vector.tensor_tensor(f_sq[:, :, :], f_cent[:, :, :], f_cent[:, :, :], ALU.mult).then_inc(f_dve, 1)

            def f_scale(dst, m, n_pe, gamma, beta, eps):
                dve.wait_ge(f_pe, n_pe)
                nc.vector.tensor_scalar(fve[:, :], F_VAR, eps, None, ALU.add).then_inc(f_ve, 1)
                if gamma is None:
                    dve.wait_ge(f_pool, m + 1)
                    nc.vector.tensor_tensor(dst[:, :, :], f_cent[:, :, :], over_rows(frs[:, :]), ALU.mult).then_inc(f_dve, 1)
                    return
                nc.vector.tensor_tensor(f_sc[:, :, :], f_cent[:, :, :], gamma, ALU.mult).then_inc(f_gam, 1)
                dve.wait_ge(f_pool, m + 1)
                dve.wait_ge(f_gam, m)
                link(nc.vector.tensor_tensor(f_sc[:, :, :], f_sc[:, :, :], over_rows(frs[:, :]), ALU.mult))
                nc.vector.tensor_tensor(dst[:, :, :], f_sc[:, :, :], beta, ALU.add).then_inc(f_dve, 1)

            def step_center(k):
                f_center(th[:, :, :], 6 + 4 * k)
                nc.vector.tensor_tensor(thb[:, :, :], th[:, :, :], d2_b, ALU.add).then_inc(f_thb, 1)

            def step_scale(k):
                f_scale(f_t, 2 + k, 7 + 4 * k, pn_gamma, pn_beta, EPS_N)

            def step_hidden(k):
                dve.wait_ge(f_pe, 8 + 4 * k)
                nc.vector.tensor_tensor(zz[:, :, :], F_D1,
                                        d1_b.unsqueeze(2).to_broadcast([128, HC, 2]), ALU.add).then_inc(f_dve, 1)

            def step_thought(k):
                dve.wait_ge(f_thb, k + 1)
                dve.wait_ge(f_pe, 9 + 4 * k)
                nc.vector.tensor_tensor(th[:, :, :], F_TH, thb[:, :, :],
                                        ALU.add).then_inc(f_dve, 1)

            def copy_thought():
                dve.wait_ge(f_dve, 5 + 4 * K_STEPS)
                nc.vector.tensor_copy(thB[:, :, :, :], th[:, :, :].rearrange("p c b -> p b c").unsqueeze(3)
                                      .to_broadcast([128, BATCH, DC, 128])).then_inc(f_dve, 1)

            def broadcast_half():
                dve.wait_ge(l_bcb, 16)
                link(nc.vector.tensor_scalar(bcb, bcb, 0.5, None, ALU.mult))
                dve.wait_ge(f_pe, 6 + 4 * K_STEPS)
                link(nc.vector.scalar_tensor_tensor(out=hb[:, :, :], in0=OU[:, :].rearrange("p (b d) -> p b d", b=BATCH),
                                                    scalar=0.5, in1=bcb.unsqueeze(1).to_broadcast([128, BATCH, D]),
                                                    op0=ALU.mult, op1=ALU.add))

            def gate_bias():
                dve.wait_ge(l_gb, 32)
                dve.wait_ge(p_init, 5)
                link(nc.vector.tensor_copy(gbh[32:33, :], gbr[32:33, :]))
                nc.vector.tensor_copy(gb_part[0:1, :], gbr[0:1, :])
                nc.vector.tensor_tensor(gb_part[32:33, :], gbr[32:33, :], gbh[32:33, :].bitcast(F32), ALU.subtract)
                nc.vector.memset(gb_sel[0:1, :].bitcast(F32), 1.0)
                nc.vector.memset(gb_sel[32:33, :].bitcast(F32), 1.0).then_inc(d_one, 3)

            w1 = bc128[:, 2 * D:2 * D + 2 * DH]

            def rope_weights():
                dve.wait_ge(l_b128, 16)
                nc.vector.tensor_scalar(w1[:, 0:DH], w1[:, 0:DH], 1.0, None, ALU.add)
                link(nc.vector.tensor_scalar(w1[:, DH:2 * DH], w1[:, DH:2 * DH], 1.0, DH ** 0.5, ALU.add, ALU.mult))

            def rope_table(part, q, loaded):
                dve.wait_ge(loaded, 16)
                w = w1[:, DH * q:DH * q + DH].rearrange("p (a d) -> p a d", a=2)
                if part:
                    w = w[:, ::-1, :]
                tab = ((cosq, cosk), (sinq, sink))[part][q]
                raw = quarter[2 + part].rearrange("p (m a d) -> p m a d", a=2, d=DH // 2)
                return nc.vector.tensor_tensor(tab[:, :, :].rearrange("p m (a d) -> p m a d", a=2), raw,
                                               w.unsqueeze(1).to_broadcast([128, TPB, 2, DH // 2]), ALU.mult)

            dve.wait_ge(l_cols, 16)
            f_center(x_last, 1)
            dve.wait_ge(l_x[0], 16)
            link(nc.vector.bn_stats(lst[:, :], xt[0][:, :]))
            nc.vector.bn_aggr(lmv[:, :], lst[:, :]).then_inc(d_lmv, 1)
            f_scale(th, 0, 2, None, None, EPS_X)
            x_norm(0, 0)
            f_center(th[:, :, :], 3)
            f_scale(f_t, 1, 4, in_gamma, in_beta, EPS_N)
            dve.wait_ge(l_ident, 16)
            nc.vector.tensor_copy(identb[:, :], identf[:, :]).then_inc(d_one, 1)
            dve.wait_ge(f_pe, 5)
            nc.vector.tensor_tensor(th[:, :, :], F_TH, agg_b, ALU.add).then_inc(f_dve, 1)
            step_center(0)
            step_scale(0)
            gate_bias()
            w_lo(0)
            w_lo(1)
            rope_weights()
            step_hidden(0)
            rope_table(0, 0, l_cos)
            rope_table(0, 1, l_cos)
            rope_table(1, 0, l_sin)
            rope_table(1, 1, l_sin).then_inc(d_tab, 1)
            step_thought(0)

            def rotate(dst_c, dst_s, bank, cos, sin, m):
                c = cos[:, bass.ds(m, 1), :].to_broadcast([128, 4, DH])
                q = sin[:, bass.ds(m, 1), :].rearrange("p m (a d) -> p m a d", a=2).to_broadcast([128, 4, 2, DH // 2])
                nc.vector.tensor_tensor(dst_c.rearrange("p (h d) -> p h d", h=4),
                                        bank.rearrange("p (h d) -> p h d", h=4), c, ALU.mult)
                return nc.vector.tensor_tensor(dst_s.rearrange("p (h a d) -> p h a d", h=4, a=2),
                                               bank.rearrange("p (h a d) -> p h a d", h=4, a=2)[:, :, ::-1, :], q,
                                               ALU.mult)

            def slot(i, k, s):
                par, j, n = k // 4, k % 4, 2 * i + k // 4
                if j == 0 and tile_exists(n):
                    x_lo(n, par)
                if isinstance(s, int) and s == 0:
                    step_center(1)
                    for c in range(2, 6):
                        w_lo(c)
                    step_scale(1)
                    for c in range(6, NW):
                        w_lo(c)
                    dve.wait_ge(d_tab, 1)
                if exists(s, 3):
                    t = s - 3
                    dve.wait_ge(a_exp, t + 1)
                    wait(dve, p_norm, t - 1)
                    nc.vector.reciprocal(rinv[(k - 3) % 2][:, :], rsum[(k - 3) % 2][:, :]).then_inc(d_rinv, 1)
                if exists(s, 1):
                    t = s - 1
                    jt, pt = (k - 1) % 4, ((k - 1) // 4) % 2
                    it = i if k >= 1 else i - 1
                    nt = 2 * it + pt
                    dve.wait_ge(pe_pa, JOBS * nt + Q_P[jt] + 1)
                    wait(dve, pe_T, t - 1)
                    rotate(t1[(k - 1) % 2], t2[(k - 1) % 2], PA[(pt + Q_P[jt]) % 2][:, :], cosq, sinq,
                           (it % 4) * 2 + pt).then_inc(d_rope, 1)
                if isinstance(s, int) and s in (2, 3):
                    step_center(s)
                if isinstance(s, int) and s == 2:
                    step_scale(2)
                if isinstance(s, int) and s == 4:
                    broadcast_half()
                if j == 0 and tile_exists(n - 1):
                    it = i if par else i - 1
                    dve.wait_ge(a_gate, n)
                    wait(dve, p_gy, n - 1)
                    nc.vector.scalar_tensor_tensor(out=gu[:, :], in0=gth[:, :], scalar=1.0,
                                                   in1=hb[:, bass.ds(it // 4, 1), :].rearrange("p b d -> p (b d)"),
                                                   op0=ALU.add, op1=ALU.mult).then_inc(d_gu, 1)
                if j == 1 and tile_exists(n):
                    dve.wait_ge(pe_pa, JOBS * n + Q_K + 1)
                    wait(dve, pe_kT, n)
                    rotate(kt1[:, :], kt2[:, :], PA[(par + Q_K) % 2][:, :], cosk, sink, (i % 4) * 2 + par)\
                        .then_inc(d_krope, 1)
                if exists(s, 4):
                    t = s - 4
                    dve.wait_ge(a_ct, t + 1)
                    nc.vector.tensor_tensor(cT[k % 2][:, 1].rearrange("p h u t -> p u h t"),
                                            CT[:, :].rearrange("p (u h t) -> p u h t", u=2, h=G),
                                            cT[k % 2][:, 0].rearrange("p h u t -> p u h t").bitcast(F32),
                                            ALU.subtract).then_inc(d_ct, 1)
                if exists(s, 2):
                    t = s - 2
                    dve.wait_ge(pe_S, t + 1)
                    wait(dve, a_exp, t - 1)
                    nc.vector.tensor_reduce(nmx[k % 2][:, :], SC[k % 2][:, :].rearrange("p (c n) -> p c n", c=4), AX.X,
                                            ALU.max, negate=True).then_inc(d_mx, 1)
                if j == 1 and tile_exists(n):
                    dve.wait_ge(d_krope, n + 1)
                    nc.vector.tensor_tensor(kt1[:, :], kt1[:, :], kt2[:, :], ALU.add).then_inc(d_kadd, 1)
                if j == 2 and tile_exists(n):
                    dve.wait_ge(a_vhi, n + 1)
                    nc.vector.tensor_tensor(Va[par][:, 1, :], PA[(par + Q_V) % 2][:, :], Va[par][:, 0, :].bitcast(F32),
                                            ALU.subtract).then_inc(d_vlo, 1)
                if exists(s, 2):
                    dve.wait_ge(p_r, t + 1)
                    for hh in range(2):
                        for u in range(2):
                            last = nc.vector.tensor_copy(r2[k % 2][64 * hh:64 * hh + 64, :, u],
                                                         rq[k % 2][64 * u:64 * u + 64, hh::2])
                    last.then_inc(d_r2, 1)
                    dve.wait_ge(d_mx, t + 1)
                    dve.wait_ge(d_r2, t + 1)
                    nc.vector.tensor_tensor(nb[k % 2][:, :], nmx[k % 2][:, :],
                                            r2[k % 2][:, :, :].rearrange("p a u -> p (a u)"), ALU.mult).then_inc(d_nb, 1)
                if exists(s, 3):
                    t = s - 3
                    dve.wait_ge(a_pt, t + 1)
                    nc.vector.tensor_tensor(pT[(k - 3) % 2][:, 1],
                                            TR[0 if j >= 2 else 1][:, :].rearrange("p (a u c) -> p a u c", a=2, u=2),
                                            pT[(k - 3) % 2][:, 0].bitcast(F32), ALU.subtract).then_inc(d_pt, 1)
                if isinstance(s, int) and s == 3:
                    step_scale(3)
                if isinstance(s, int) and s in (1, 2, 3):
                    step_hidden(s)
                if j == 0 and (not isinstance(n, int) or (2 <= n < TILES + 2)):
                    dve.wait_ge(a_silu, n - 1)
                    wait(dve, d_out, n - 2)
                    nc.vector.scalar_tensor_tensor(out=gg[:, :], in0=gsl[:, :], scalar=1.0, in1=gz[:, :],
                                                   op0=ALU.add, op1=ALU.mult).then_inc(d_gg, 1)
                    dve.wait_ge(pe_O, 4 * n - 4)
                    dve.wait_ge(d_gg, n - 1)
                    wait(dve, p_fin, n - 2)
                    nc.vector.scalar_tensor_tensor(out=so[:, :], in0=OU[:, 0:D], scalar=0.5,
                                                   in1=gg[:, :], op0=ALU.mult, op1=ALU.mult).then_inc(d_out, 1)
                if j == 0 and tile_exists(n + 1):
                    dve.wait_ge(l_x[1 - par], 16 * (i + 1 + par))
                    dve.wait_ge(d_xn, n + 1)
                    x_stats(n + 1, 1 - par)
                if j == 1 and tile_exists(n - 1):
                    dve.wait_ge(p_gy, n)
                    wait(dve, d_g2, n - 1)
                    nc.vector.bn_stats(gst[:, :], gy[:, :]).then_inc(d_gst, 1)
                    dve.wait_ge(l_x[0], 16)
                    dve.wait_ge(d_gst, n)
                    nc.vector.bn_aggr(gmv[:, :], gst[:, :]).then_inc(d_gmv, 1)
                if j == 2 and tile_exists(n + 1):
                    if later(n, 1):
                        dve.wait_ge(p_gy, n)
                    x_norm(n + 1, 1 - par)
                if j == 3 and tile_exists(n - 1):
                    dve.wait_ge(p_grs, n)
                    dve.wait_ge(d_gmv, n)
                    wait(dve, d_gg, n - 1)
                    nc.vector.scalar_tensor_tensor(out=gz[:, :], in0=gy[:, :], scalar=gmv[:, 0:1], in1=out_gamma,
                                                   op0=ALU.subtract, op1=ALU.mult).then_inc(d_g1, 1)
                    dve.wait_ge(d_g1, n)
                    nc.vector.scalar_tensor_tensor(out=gz[:, :], in0=gz[:, :], scalar=grs[:, 0:1], in1=out_beta,
                                                   op0=ALU.mult, op1=ALU.add).then_inc(d_g2, 1)
                if isinstance(s, int) and s in (1, 2, 3):
                    step_thought(s)
                if isinstance(s, int) and s == 3:
                    copy_thought()
            program(nc.vector, slot)


def kernel(**inputs):
    import numpy as np
    import ml_dtypes
    import concourse.bacc as bacc
    from concourse.bass_utils import run_bass_kernel_spmd as run

    a = {k.replace("L0_attn_", "").replace("L0_ffn_", "f_"): np.asarray(v) for k, v in inputs.items()}

    def parts(w, c=DC):
        return np.ascontiguousarray(w.reshape(c, 128, -1).transpose(1, 0, 2))

    def col(v):
        return v.reshape(-1, 128).T

    arrays = {
        "x": np.ascontiguousarray(a["x"]),
        "wq": np.ascontiguousarray(a["Wq"].T.reshape(DC, 128, KV, 512).transpose(1, 2, 0, 3)),
        "wk": parts(a["Wk"].T),
        "wv": parts(a["Wv"].T),
        "wo": parts(a["Wo"].T, HEADS),
        "gw": parts(a["f_gate_w"]),
        "aggw": parts(a["f_agg_w"]),
        "d1w": parts(a["f_d1_w"]),
        "d2w": parts(a["f_d2_w"], HC),
        "bcw": parts(a["f_bc_w"]),
        "cols": np.ascontiguousarray(np.concatenate(
            [col(a["f_" + k]) for k in ("d1_b", "in_gamma", "in_beta", "pn_gamma", "pn_beta", "agg_b", "d2_b")]
            + [a["x"][:, T - 1, :].reshape(BATCH, DC, 128).transpose(2, 1, 0).reshape(128, -1)], axis=1)),
        "bcrow": a["f_bc_b"],
        "rows128": np.concatenate([a["f_out_gamma"], a["f_out_beta"], a["qn_w"], a["kn_w"]]),
        "gbrow": np.ascontiguousarray(a["f_gate_b"].reshape(1, D)),
    }
    inv = np.float32(1.0) / np.float32(10000.0) ** (np.arange(0, DH, 2, dtype=np.float32) / np.float32(DH))
    ang = np.arange(T, dtype=np.float32)[:, None] * inv[None, :].astype(np.float32)
    cos, sin = np.cos(ang), np.sin(ang)
    rope = np.stack([np.concatenate([cos, cos], 1), np.concatenate([-sin, sin], 1)])
    arrays["rope"] = np.ascontiguousarray(rope.reshape(2, TPB, 128, DH).transpose(2, 0, 1, 3).astype(np.float32))
    tok, key = np.arange(128)[:, None] % 64, np.arange(128)[None, :]
    second = (key >= tok) & (key <= tok + WINDOW)
    before = (key >= 64) & (key >= tok + 64)
    same = (key < 64) & (key <= tok)
    masks = np.stack([np.stack([same, second]), np.stack([same | before, second])])
    arrays["masks"] = np.ascontiguousarray(
        np.where(masks, 0.0, -1e30).transpose(2, 0, 1, 3).astype(ml_dtypes.bfloat16))
    arrays["ident"] = np.eye(128, dtype=np.float32)

    nc = bacc.Bacc("TRN2", target_bir_lowering=False, num_devices=1)
    aps = {k: nc.dram_tensor(k, v.shape, mybir.dt.from_np(v.dtype), kind="ExternalInput").ap()
           for k, v in arrays.items()}
    out = nc.dram_tensor("out", (BATCH, T, D), F32, kind="ExternalOutput").ap()
    build(nc, out=out, **aps)
    return run(nc, [arrays], core_ids=[0]).results[0]["out"]
```
